# Optimizing a Trainium2 kernel written in Bass

```python
import numpy as np
import jax
import jax.numpy as jnp

def _softmax(x, axis=-1):
    return jax.nn.softmax(x, axis=axis)

def _gelu(x):
    return jax.nn.gelu(x, approximate=True)

def _silu(x):
    return jax.nn.silu(x)

def _sigmoid(x):
    return jax.nn.sigmoid(x)

def _layernorm(x, axis=-1, eps=1e-05):
    m = jnp.mean(x, axis=axis, keepdims=True)
    v = jnp.var(x, axis=axis, keepdims=True)
    return (x - m) / jnp.sqrt(v + eps)

def _scatter_add(tgt, idx, src, axis=0):
    return tgt.at[idx].add(src)

def _segment_sum(src, seg, n):
    return jax.ops.segment_sum(src, seg, n)
kernel_name = 'mk_flamingo_gated_d2_seqx_r8_cee5df'

def setup_inputs(seed: int=0):
    np.random.seed(seed)
    _w = jnp.asarray

    def _rec_inputs():
        import jax
        import jax.numpy as jnp
        _rk = jax.random.key(seed)
        x = 7.22e-05 + 1 * jax.random.normal(jax.random.fold_in(_rk, 1), (4, 256, 128), jnp.float32)
        _lenS = 256 - jax.random.randint(jax.random.fold_in(_rk, 7), (4,), 0, max(1, 256 // 4) + 1, jnp.int32)
        _lenS2 = 64 - jax.random.randint(jax.random.fold_in(_rk, 8), (4,), 0, max(1, 64 // 4) + 1, jnp.int32)
        _ctx_1024P = jax.random.normal(jax.random.fold_in(_rk, 11), (4, 16, 128), jnp.float32)
        _ctx_1024c = jax.random.dirichlet(jax.random.fold_in(_rk, 511), 0.3 * jnp.ones((16,), jnp.float32), (4, 64))
        _ctx_1024t = jnp.einsum('bsk,bkd->bsd', _ctx_1024c, _ctx_1024P)
        _ctx_1024t = _ctx_1024t * jax.lax.rsqrt(jnp.mean(jnp.square(_ctx_1024t)) + 1e-12) * 0.953939
        ctx_1024 = 4.13588e-05 + 0.999923 * (_ctx_1024t + 0.3 * jax.random.normal(jax.random.fold_in(_rk, 611), (4, 64, 128), jnp.float32))
        _g = jax.random.normal(jax.random.fold_in(_rk, 9001), (2, 2), jnp.float32)
        _g = jnp.sign(_g) * jnp.maximum(jnp.abs(_g), 1.0) + (_g == 0) * 1.0
        g_xattn = _g[0]
        g_ffn = _g[1]
        return (x, ctx_1024, g_xattn, g_ffn)
    x, ctx_1024, g_xattn, g_ffn = _rec_inputs()

    def _L0_xattn_setup():
        import jax, jax.numpy as jnp
        import numpy as np
        B, SQ, SK, D = (4, 256, 256, 128)
        key = jax.random.key(seed)
        ks = jax.random.split(key, 8)
        s = 1.0 / np.sqrt(D)
        return {'input_seq': jax.random.normal(ks[0], (B, SQ, D), jnp.float32), 'condition_seq': jax.random.normal(ks[1], (B, SK, D), jnp.float32), 'Wq': jax.random.normal(ks[2], (D, D), jnp.float32) * s, 'bq': jnp.zeros((D,), jnp.float32), 'Wk': jax.random.normal(ks[3], (D, D), jnp.float32) * s, 'bk': jnp.zeros((D,), jnp.float32), 'Wv': jax.random.normal(ks[4], (D, D), jnp.float32) * s, 'bv': jnp.zeros((D,), jnp.float32)}
    _L0_xattn_all = _L0_xattn_setup()
    _L0_xattn_in = {k: v for k, v in _L0_xattn_all.items() if k in ('Wq', 'bq', 'Wk', 'bk', 'Wv', 'bv')}
    del _L0_xattn_all

    def _L0_ffn_setup():
        import jax, jax.numpy as jnp
        import numpy as np
        B, S, H, E, K = (4, 256, 128, 8, 2)
        key = jax.random.key(seed)
        k0, k1, k2, k3 = jax.random.split(key, 4)
        x = jax.random.normal(k0, (B, S, H), dtype=jnp.float32)
        router_w = jax.random.normal(k1, (E, H), dtype=jnp.float32) * np.float32(1.0 / np.sqrt(H))
        xav1 = np.float32(np.sqrt(2.0 / (2 * H + H)))
        w1 = jax.random.normal(k2, (E, 2 * H, H), dtype=jnp.float32) * xav1
        w2 = jax.random.normal(k3, (E, H, 2 * H), dtype=jnp.float32) * xav1
        return {'x': x, 'router_w': router_w, 'w1': w1, 'w2': w2}
    _L0_ffn_all = _L0_ffn_setup()
    _L0_ffn_in = {k: v for k, v in _L0_ffn_all.items() if k in ('router_w', 'w1', 'w2')}
    del _L0_ffn_all

    def _L1_xattn_setup():
        import jax, jax.numpy as jnp
        import numpy as np
        B, T, C, H = (4, 512, 128, 16)
        D = C // H

        def _heads(t):
            b, n, c = t.shape
            return t.reshape(b, n, H, D).transpose(0, 2, 1, 3)
        key = jax.random.key(seed)
        ks = jax.random.split(key, 10)
        s = 1.0 / np.sqrt(C)
        return {'x': jax.random.normal(ks[0], (B, T, C), jnp.float32), 'y': jax.random.normal(ks[1], (B, T, C), jnp.float32), 'Wq': jax.random.normal(ks[2], (C, C), jnp.float32) * s, 'bq': jnp.zeros((C,), jnp.float32), 'Wk': jax.random.normal(ks[3], (C, C), jnp.float32) * s, 'bk': jnp.zeros((C,), jnp.float32), 'Wv': jax.random.normal(ks[4], (C, C), jnp.float32) * s, 'bv': jnp.zeros((C,), jnp.float32), 'Wp': jax.random.normal(ks[5], (C, C), jnp.float32) * s, 'bp': jnp.zeros((C,), jnp.float32)}
    _L1_xattn_all = _L1_xattn_setup()
    _L1_xattn_in = {k: v for k, v in _L1_xattn_all.items() if k in ('Wq', 'bq', 'Wk', 'bk', 'Wv', 'bv', 'Wp', 'bp')}
    del _L1_xattn_all

    def _L1_ffn_setup():
        import jax, jax.numpy as jnp
        import numpy as np
        BLOCK = 32
        W_BITS = 4
        ACT_BITS = 16

        def act_qdq(x):
            qmax = 2.0 ** (ACT_BITS - 1) - 1.0
            scale = jnp.maximum(jnp.max(jnp.abs(x)) / qmax, 1e-12)
            return jnp.clip(jnp.round(x / scale), -qmax - 1.0, qmax) * scale

        def fixed_qdq_u16(x):
            scale = 1.0 / 65536.0
            return jnp.clip(jnp.round(x / scale), 0.0, 65535.0) * scale

        def lpbq_dequant(w):
            O, I = w.shape
            qmax = 2.0 ** (W_BITS - 1) - 1.0
            wb = w.reshape(O, I // BLOCK, BLOCK)
            s = jnp.maximum(jnp.max(jnp.abs(wb), axis=-1, keepdims=True) / qmax, 1e-12)
            wq = jnp.clip(jnp.round(wb / s), -qmax - 1.0, qmax) * s
            return wq.reshape(O, I)
        key = jax.random.key(seed)
        k1, k2, k3, k4 = jax.random.split(key, 4)
        B, S, H, I = (2, 512, 128, 384)
        x = jax.random.normal(k1, (B, S, H), jnp.float32)
        w_gate = jax.random.normal(k2, (I, H), jnp.float32) * 0.02
        w_up = jax.random.normal(k3, (I, H), jnp.float32) * 0.02
        w_down = jax.random.normal(k4, (H, I), jnp.float32) * 0.02
        return {'x': x, 'w_gate': w_gate, 'w_up': w_up, 'w_down': w_down}
    _L1_ffn_all = _L1_ffn_setup()
    _L1_ffn_in = {k: v for k, v in _L1_ffn_all.items() if k in ('w_gate', 'w_up', 'w_down')}
    del _L1_ffn_all
    return {'x': x, 'ctx_1024': ctx_1024, 'g_xattn': g_xattn, 'g_ffn': g_ffn, 'L0_xattn_Wq': _L0_xattn_in['Wq'], 'L0_xattn_bq': _L0_xattn_in['bq'], 'L0_xattn_Wk': _L0_xattn_in['Wk'], 'L0_xattn_bk': _L0_xattn_in['bk'], 'L0_xattn_Wv': _L0_xattn_in['Wv'], 'L0_xattn_bv': _L0_xattn_in['bv'], 'L0_ffn_router_w': _L0_ffn_in['router_w'], 'L0_ffn_w1': _L0_ffn_in['w1'], 'L0_ffn_w2': _L0_ffn_in['w2'], 'L1_xattn_Wq': _L1_xattn_in['Wq'], 'L1_xattn_bq': _L1_xattn_in['bq'], 'L1_xattn_Wk': _L1_xattn_in['Wk'], 'L1_xattn_bk': _L1_xattn_in['bk'], 'L1_xattn_Wv': _L1_xattn_in['Wv'], 'L1_xattn_bv': _L1_xattn_in['bv'], 'L1_xattn_Wp': _L1_xattn_in['Wp'], 'L1_xattn_bp': _L1_xattn_in['bp'], 'L1_ffn_w_gate': _L1_ffn_in['w_gate'], 'L1_ffn_w_up': _L1_ffn_in['w_up'], 'L1_ffn_w_down': _L1_ffn_in['w_down']}

def reference(x, ctx_1024, g_xattn, g_ffn, L0_xattn_Wq, L0_xattn_bq, L0_xattn_Wk, L0_xattn_bk, L0_xattn_Wv, L0_xattn_bv, L0_ffn_router_w, L0_ffn_w1, L0_ffn_w2, L1_xattn_Wq, L1_xattn_bq, L1_xattn_Wk, L1_xattn_bk, L1_xattn_Wv, L1_xattn_bv, L1_xattn_Wp, L1_xattn_bp, L1_ffn_w_gate, L1_ffn_w_up, L1_ffn_w_down):
    import jax
    import jax.numpy as jnp

    def _L0_xattn_ref(input_seq, condition_seq, Wq, bq, Wk, bk, Wv, bv):
        import jax, jax.numpy as jnp
        import numpy as np
        B, SQ, SK, D = (4, 256, 256, 128)
        q = jnp.einsum('bsd,ed->bse', input_seq, Wq) + bq
        k = jnp.einsum('btd,ed->bte', condition_seq, Wk) + bk
        v = jnp.einsum('btd,ed->bte', condition_seq, Wv) + bv
        scores = jnp.einsum('bse,bte->bst', q, k)
        attn = jax.nn.softmax(scores, axis=-1)
        attended = jnp.einsum('bst,bte->bse', attn, v)
        return attended

    def _L0_ffn_ref(x, router_w, w1, w2):
        import jax, jax.numpy as jnp
        import numpy as np
        B, S, H, E, K = (4, 256, 128, 8, 2)
        bsz, seq, hidden = x.shape
        n_experts = w1.shape[0]
        tokens = x.reshape(-1, hidden)
        T = tokens.shape[0]
        logits = tokens @ router_w.T
        topv, topi = jax.lax.top_k(logits, K)
        w = jax.nn.softmax(topv, axis=-1).astype(tokens.dtype)
        gate = jnp.zeros((T, n_experts), tokens.dtype).at[jnp.arange(T)[:, None], topi].add(w)
        out = jnp.zeros_like(tokens)
        for e in range(n_experts):
            h = jax.nn.gelu(tokens @ w1[e].T, approximate=False)
            y = h @ w2[e].T
            out = out + gate[:, e:e + 1] * y
        return out.reshape(bsz, seq, hidden)

    def _L1_xattn_ref(x, y, Wq, bq, Wk, bk, Wv, bv, Wp, bp):
        import jax, jax.numpy as jnp
        import numpy as np
        B, T, C, H = (4, 512, 128, 16)
        D = C // H

        def _heads(t):
            b, n, c = t.shape
            return t.reshape(b, n, H, D).transpose(0, 2, 1, 3)
        q = jax.nn.softmax(_heads(x @ Wq.T + bq), axis=-1)
        k = jax.nn.softmax(_heads(y @ Wk.T + bk), axis=-1)
        v = _heads(y @ Wv.T + bv)
        k_cumsum = jnp.sum(k, axis=-2, keepdims=True)
        D_inv = 1.0 / jnp.sum(q * k_cumsum, axis=-1, keepdims=True)
        kv = jnp.einsum('bhnd,bhne->bhde', k, v)
        out = q + jnp.einsum('bhnd,bhde->bhne', q, kv) * D_inv
        out = out.transpose(0, 2, 1, 3).reshape(x.shape[0], x.shape[1], C)
        return out @ Wp.T + bp

    def _L1_ffn_ref(x, w_gate, w_up, w_down):
        import jax, jax.numpy as jnp
        import numpy as np
        BLOCK = 32
        W_BITS = 4
        ACT_BITS = 16

        def act_qdq(x):
            qmax = 2.0 ** (ACT_BITS - 1) - 1.0
            scale = jnp.maximum(jnp.max(jnp.abs(x)) / qmax, 1e-12)
            return jnp.clip(jnp.round(x / scale), -qmax - 1.0, qmax) * scale

        def fixed_qdq_u16(x):
            scale = 1.0 / 65536.0
            return jnp.clip(jnp.round(x / scale), 0.0, 65535.0) * scale

        def lpbq_dequant(w):
            O, I = w.shape
            qmax = 2.0 ** (W_BITS - 1) - 1.0
            wb = w.reshape(O, I // BLOCK, BLOCK)
            s = jnp.maximum(jnp.max(jnp.abs(wb), axis=-1, keepdims=True) / qmax, 1e-12)
            wq = jnp.clip(jnp.round(wb / s), -qmax - 1.0, qmax) * s
            return wq.reshape(O, I)
        x = act_qdq(x)
        up = act_qdq(x @ lpbq_dequant(w_up).T)
        gate = act_qdq(x @ lpbq_dequant(w_gate).T)
        sig = fixed_qdq_u16(jax.nn.sigmoid(gate))
        gate = act_qdq(gate * sig)
        o = act_qdq(gate * up)
        return o @ lpbq_dequant(w_down).T
    x = x + jnp.tanh(g_xattn[0]) * _L0_xattn_ref(_layernorm(x, axis=-1), ctx_1024, L0_xattn_Wq, L0_xattn_bq, L0_xattn_Wk, L0_xattn_bk, L0_xattn_Wv, L0_xattn_bv)
    x = x + jnp.tanh(g_ffn[0]) * _L0_ffn_ref(_layernorm(x, axis=-1), L0_ffn_router_w, L0_ffn_w1, L0_ffn_w2)
    x = x + jnp.tanh(g_xattn[1]) * _L1_xattn_ref(_layernorm(x, axis=-1), ctx_1024, L1_xattn_Wq, L1_xattn_bq, L1_xattn_Wk, L1_xattn_bk, L1_xattn_Wv, L1_xattn_bv, L1_xattn_Wp, L1_xattn_bp)
    x = x + jnp.tanh(g_ffn[1]) * _L1_ffn_ref(_layernorm(x, axis=-1), L1_ffn_w_gate, L1_ffn_w_up, L1_ffn_w_down)
    return x

_drawn_inputs = setup_inputs


def setup_inputs(seed=0):
    import zlib

    import numpy as np

    out = dict(_drawn_inputs(seed))
    spreads = {'g_ffn': (-1.0, 0.6),
     'L0_xattn_bq': (0.0, 0.1),
     'L0_xattn_bk': (0.0, 0.8),
     'L0_xattn_bv': (0.0, 0.1),
     'L1_xattn_bq': (0.0, 0.8),
     'L1_xattn_bk': (0.0, 0.8),
     'L1_xattn_bv': (0.0, 0.1),
     'L1_xattn_bp': (0.0, 0.1)}
    factors = {'L1_ffn_w_gate': 8.0, 'L1_ffn_w_up': 8.0, 'L1_ffn_w_down': 8.0}
    for name, (base, spread) in spreads.items():
        noise = np.random.default_rng([zlib.crc32(name.encode()), seed]).standard_normal(out[name].shape)
        drawn = base * np.exp(spread * noise) if base else spread * noise
        out[name] = jnp.asarray(drawn.astype(out[name].dtype))
    for name, factor in factors.items():
        out[name] = (out[name] * factor).astype(out[name].dtype)
    return out
```

```python
import numpy as np

D = 128
BATCH, SEQ, CTX = 4, 256, 64
TOKENS = BATCH * SEQ
HALVES = 2
HT = TOKENS // HALVES
TILES = HT // D
BPH = BATCH // HALVES
TPB = SEQ // D
EXPERTS = 8
FC = 2
HEADS, HD = 16, 8
INTER = 384
IC = INTER // D
QBLOCK = 32
NBLK = D // QBLOCK
LN_EPS = 1e-5
QMAX = 32767.0
WQMAX = 7.0
QMIN_SCALE = 1e-12
SIG_STEPS = 65536.0
ROUND = 1.5 * 2.0 ** 23

PA = {"wq": 0, "wkT": 128, "wvT": 256, "ctxT": 384, "rwT": 640, "bq": 648, "bk": 649}
PA_COLS = 650
PB = {"wqT": 0, "wkT": 128, "wvT": 256, "wpT": 384}
PB_COLS = 512
ROW = {"bv0": 0, "bq1": 128, "bk1": 256, "bv1": 384, "bp1": 512, "g": 640}
ROW_COLS = 644
G_XATTN0, G_XATTN1, G_FFN0, G_FFN1 = 0, 1, 2, 3


def build(nc, x, packa, packb, rows, experts, lpbq, out):
    import concourse.bass as bass
    from concourse import mybir
    from contextlib import ExitStack

    f32, f32r, bf16 = mybir.dt.float32, mybir.dt.float32r, mybir.dt.bfloat16
    i16, u16 = mybir.dt.int16, mybir.dt.uint16
    ACT = mybir.ActivationFunctionType
    ALU = mybir.AluOpType
    X = mybir.AxisListType.X

    ctx = ExitStack()
    with ctx:
        def sb(name, shape, dt=f32):
            return ctx.enter_context(nc.sbuf_tensor(name, shape, dt))

        def sem(name):
            return ctx.enter_context(nc.semaphore(name))

        bank = [ctx.enter_context(nc.psum_tensor(f"bank{i}", [128, 512], f32)) for i in range(8)]

        xin = sb("xin", [128, 8, D])
        pa = sb("pa", [128, PA_COLS])
        pb = sb("pb", [128, PB_COLS])
        row = sb("row", [1, ROW_COLS])
        wexp = sb("wexp", [128, EXPERTS * 512])
        wq4 = sb("wq4", [128, 3 * IC, D])

        def A(name, n):
            return pa[:, PA[name]:PA[name] + n]

        def B(name):
            return pb[:, PB[name]:PB[name] + D]

        def R(name, n=D):
            return row[0:1, ROW[name]:ROW[name] + n]

        ident = sb("ident", [128, 128])
        identb = sb("identb", [128, 128], bf16)
        ones = sb("ones", [128, 256])
        zerob = sb("zerob", [128, 512], bf16)
        head_mask = sb("head_mask", [128, HEADS, HD])
        rank = sb("rank", [128, EXPERTS])
        sel = sb("sel", [128, EXPERTS, 128], bf16)
        neg_half = sb("neg_half", [128, TILES])

        kT = sb("kT", [128, BATCH * CTX])
        wqk = sb("wqk", [128, BATCH * CTX])
        bqk = sb("bqk", [1, BATCH * CTX])
        v0 = sb("v0", [CTX, BATCH, D])
        k1 = sb("k1", [CTX, BATCH, D])
        k1e = sb("k1e", [CTX, BATCH, D])
        v1 = sb("v1", [CTX, BATCH, D])
        k1max = sb("k1max", [CTX, BATCH * HEADS])
        k1sum = sb("k1sum", [CTX, BATCH * HEADS])
        kv_raw = sb("kv_raw", [128, BATCH, D])
        kv = sb("kv", [128, BATCH, D])
        ksum = sb("ksum", [128, BATCH])
        kc = sb("kc", [128, BATCH, HEADS])
        tg = sb("tg", [128, 4])

        stats = sb("stats", [128, TILES, 6])
        mv = sb("mv", [128, TILES, 2])
        var = sb("var", [128, TILES])
        rstd = sb("rstd", [128, TILES])
        xn = sb("xn", [128, 8, D])
        xT = sb("xT", [128, TOKENS])
        xhi = sb("xhi", [128, TOKENS], f32r)
        xlo = sb("xlo", [128, TOKENS], f32r)
        smax = sb("smax", [128, TILES])
        ssum = sb("ssum", [128, TILES])
        sc = sb("sc", [128, TILES, CTX])
        pr = sb("pr", [128, TILES, CTX])
        prT = sb("prT", [CTX, HT])
        x2 = sb("x2", [128, 8, D])
        rw_hi = sb("rw_hi", [128, EXPERTS], f32r)
        rw_lo = sb("rw_lo", [128, EXPERTS], f32r)
        lg = sb("lg", [128, TILES, EXPERTS])
        lg2 = sb("lg2", [128, TILES, EXPERTS])
        eq = sb("eq", [128, TILES, EXPERTS])
        top1 = sb("top1", [128, TILES, EXPERTS])
        top2 = sb("top2", [128, TILES, EXPERTS])
        gate = sb("gate", [128, TILES, EXPERTS])
        rest = sb("rest", [128, TILES, EXPERTS])
        m1 = sb("m1", [128, TILES])
        m2 = sb("m2", [128, TILES])
        mr = sb("mr", [128, TILES])
        ex = sb("ex", [128, TILES])
        gpart = sb("gpart", [128, 8, 128], bf16)
        gateT = sb("gateT", [128, TOKENS], bf16)
        NB = 4
        high_parts = sb("high_parts", [128, 6 * 512], f32r)
        low_parts = sb("low_parts", [128, 6 * 512], f32r)
        hidden = sb("hidden", [128, 2 * NB * 512])

        def buffers(t, first, n):
            return [t[:, k * 512:(k + 1) * 512] for k in range(first, first + n)]

        h_hi, w_hi = buffers(high_parts, 0, NB), buffers(high_parts, NB, 2)
        h_lo, w_lo = buffers(low_parts, 0, NB), buffers(low_parts, NB, 2)
        ge, hm = buffers(hidden, 0, NB), buffers(hidden, NB, NB)
        yT = xT
        x3 = sb("x3", [128, 8, D])
        qs = sb("qs", [128, 512])
        qe = sb("qe", [128, 512])
        qmax = sb("qmax", [128, TILES * HEADS])
        qsum = sb("qsum", [128, TILES * HEADS])
        qn = sb("qn", [128, 512])
        qeT = sb("qeT", [128, 512])
        dinv = sb("dinv", [128, TILES * HEADS])
        att = sb("att", [128, 512])
        ao = sb("ao", [128, 512])
        aoT = sb("aoT", [128, 512])
        x4 = sb("x4", [128, 8, D])
        x4T = sb("x4T", [128, TOKENS])
        wb_max = sb("wb_max", [128, 3 * IC * NBLK])
        wb_s = sb("wb_s", [128, 3 * IC * NBLK])
        wb_r = sb("wb_r", [128, 3 * IC * NBLK])
        wb_i = sb("wb_i", [128, 3 * IC, D])
        wb_d = wb_i
        wT = sb("wT", [128, 3 * IC, D])
        wT_hi = sb("wT_hi", [128, 3 * IC, D], f32r)
        wT_lo = sb("wT_lo", [128, 3 * IC, D], f32r)
        nx = sb("nx", [128, TOKENS], i16)
        gq = sb("gq", [128, IC, TOKENS])
        up = sb("up", [128, IC, TOKENS])
        ng = sb("ng", [128, IC, TOKENS], i16)
        def third(t, dt=None):
            t = t if dt is None else t.bitcast(dt)
            return t.rearrange("p (c n) -> p c n", c=IC)

        nu = third(wexp[:, 0:1536], i16)
        sq = third(wexp[:, 1536:3072], u16)
        sg = third(hidden[:, 0:3072])
        pg = sg
        n3 = ng
        og = gq
        n4 = nu
        o_hi = third(high_parts[:, :])
        o_lo = third(low_parts[:, :])
        res = hidden[:, 3072:4096]
        STG = ("x", "g", "u", "p", "o")
        amax = {k: sb(f"amax_{k}", [128, 6]) for k in STG}
        amax1 = {k: sb(f"amax1_{k}", [128, 1]) for k in STG}
        gmax = {k: sb(f"gmax_{k}", [128, 1]) for k in STG}
        scale = {k: sb(f"scale_{k}", [128, 1]) for k in STG}
        rcp = {k: sb(f"rcp_{k}", [128, 1]) for k in STG}
        mul = {k: sb(f"mul_{k}", [128, 1]) for k in STG}
        unit = {k: sb(f"unit_{k}", [128, 1]) for k in STG}
        unitq = {k: sb(f"unitq_{k}", [128, 1]) for k in STG}
        tscale = sb("tscale", [128, 1])
        warm = sb("warm", [1, 2])

        x_in = [sem(f"x_in{h}") for h in range(HALVES)]
        pa_in, pb_in, row_in, exp_in, lpbq_in, out_done = map(
            sem, ("pa_in", "pb_in", "row_in", "exp_in", "lpbq_in", "out_done"))
        const_ready, const_late, pool_step = map(sem, ("const_ready", "const_late", "pool_step"))
        dve_step, act_step = map(sem, ("dve_step", "act_step"))
        kT_mm, kT_ready, v0_mm, v0_ready, g_mm, tg_ready = map(
            sem, ("kT_mm", "kT_ready", "v0_mm", "v0_ready", "g_mm", "tg_ready"))
        wqk_mm, wqk_ready, kv1_mm, k1_ready, v1_ready, k1_soft = map(
            sem, ("wqk_mm", "wqk_ready", "kv1_mm", "k1_ready", "v1_ready", "k1_soft"))
        kv_mm, kv_raw_ready, kv_ready = map(sem, ("kv_mm", "kv_raw_ready", "kv_ready"))
        var_ready, rstd_ready, xn_ready, xT_mm, xT_ready = map(
            sem, ("var_ready", "rstd_ready", "xn_ready", "xT_mm", "xT_ready"))
        s_mm, s_sub, pr_ready, prT_mm, prT_ready, pv_mm, x2_ready = map(
            sem, ("s_mm", "s_sub", "pr_ready", "prT_mm", "prT_ready", "pv_mm", "x2_ready"))
        xhi_ready, xlo_ready, rw_ready, lg_mm, lg_read, dm_ready, ex_ready = map(
            sem, ("xhi_ready", "xlo_ready", "rw_ready", "lg_mm", "lg_read", "dm_ready", "ex_ready"))
        gpart_ready, gateT_mm, gateT_ready = map(sem, ("gpart_ready", "gateT_mm", "gateT_ready"))
        w1_split, w2_split, z_ready, gb_ready = map(
            sem, ("w1_split", "w2_split", "z_ready", "gb_ready"))
        gelu_done, gated, hi_done, lo_done, y_done = map(
            sem, ("gelu_done", "gated", "hi_done", "lo_done", "y_done"))
        yT_ready, yN_mm, x3_ready = map(sem, ("yT_ready", "yN_mm", "x3_ready"))
        q_mm, q_sub, qe_ready, qeT_mm, qeT_ready, qsum_ready, qn_ready = map(
            sem, ("q_mm", "q_sub", "qe_ready", "qeT_mm", "qeT_ready", "qsum_ready", "qn_ready"))
        nd_mm, ao_ready, aoT_mm, aoT_ready, proj_mm, x4_ready = map(
            sem, ("nd_mm", "ao_ready", "aoT_mm", "aoT_ready", "proj_mm", "x4_ready"))
        x4T_mm, x4T_ready, wb_scale, wb_ready, wT_mm, wT_ready, wT_split = map(
            sem, ("x4T_mm", "x4T_ready", "wb_scale", "wb_ready", "wT_mm", "wT_ready", "wT_split"))
        amax_ready = {k: sem(f"amax_ready_{k}") for k in STG}
        gmax_ready = {k: sem(f"gmax_ready_{k}") for k in STG}
        mul_ready = {k: sem(f"mul_ready_{k}") for k in STG}
        nx_ready, gu_mm, gu_ready, gu_free = map(sem, ("nx_ready", "gu_mm", "gu_ready", "gu_free"))
        ng_ready, sg_ready, sq_ready, nu_ready, n4_ready, ohi_ready, olo_ready = map(
            sem, ("ng_ready", "sg_ready", "sq_ready", "nu_ready", "n4_ready", "ohi_ready", "olo_ready"))
        dn_mm, res_ready = map(sem, ("dn_mm", "res_ready"))

        CREDIT = 8

        def half(t, h):
            return t[:, h * HT:(h + 1) * HT]

        def tiles(t, h):
            return t[:, h * TILES:(h + 1) * TILES, :]

        block = ctx.enter_context(nc.Block())

        @block.sync
        def _(sp):
            xv = x.rearrange("b (t p) d -> p (b t) d", p=128)
            sp.dma_start(xin[:, 0:TILES, :], xv[:, 0:TILES, :]).then_inc(x_in[0], 16)
            sp.dma_start(pa[:, :], packa).then_inc(pa_in, 16)
            sp.dma_start(xin[:, TILES:, :], xv[:, TILES:, :]).then_inc(x_in[1], 16)
            sp.dma_start(pb[:, :], packb).then_inc(pb_in, 16)
            sp.dma_start(wexp[:, :], experts).then_inc(exp_in, 16)
            sp.dma_start(wq4[:, :, :], lpbq).then_inc(lpbq_in, 16)
            for h in range(HALVES):
                sp.wait_ge(res_ready, h + 1)
                sp.dma_start(half(out, h), half(res, h)).then_inc(out_done, 16)
            sp.wait_ge(out_done, 16 * HALVES)

        @block.gpsimd
        def _(pool):
            steps = [0]

            def step(ins):
                steps[0] += 1
                ins.then_inc(pool_step, 1)
                return steps[0]

            pool.memset(ident[:, :], 0.0)
            pool.memset(ones[:, :], 1.0)
            n = step(pool.memset(neg_half[:, :], -0.5))
            pool.wait_ge(pool_step, n)
            n = step(pool.affine_select(out=ident[:, :], in_=ident[:, :], compare_op=ALU.not_equal, fill=1.0,
                                        base=0, pattern=[[-1, 128]], channel_multiplier=1))
            pool.wait_ge(pool_step, n)
            pool.drain().then_inc(const_ready, 1)

            def rstd_of(n):
                pool.wait_ge(var_ready, n)
                pool.tensor_tensor(rstd[:, :], var[:, :], neg_half[:, :], ALU.pow).then_inc(rstd_ready, 1)

            rstd_of(1)
            rstd_of(2)
            pool.memset(sel[:, :, :], 0.0)
            pool.memset(gpart[:, :, :], 0.0)
            pool.memset(zerob[:, :], 0.0)
            n = step(pool.iota(rank[:, :], pattern=[[-1, EXPERTS]], base=EXPERTS, channel_multiplier=0,
                               allow_small_or_imprecise_dtypes=True))
            pool.wait_ge(pool_step, n)
            for part in range(3):
                n = step(pool.affine_select(out=sel[:, :, :], in_=sel[:, :, :], compare_op=ALU.not_equal,
                                            fill=1.0, base=-EXPERTS * part,
                                            pattern=[[-1, EXPERTS], [0, 128]], channel_multiplier=1))
                pool.wait_ge(pool_step, n)
            n = step(pool.tensor_tensor(identb[:, :], ident[:, :], ident[:, :], ALU.mult))
            n = step(pool.memset(head_mask[:, :, :], 1.0))
            pool.wait_ge(pool_step, n)
            n = step(pool.affine_select(out=head_mask[:, :, :], in_=head_mask[:, :, :], compare_op=ALU.is_ge,
                                        fill=0.0, base=0, pattern=[[-HD, HEADS], [0, HD]],
                                        channel_multiplier=1))
            pool.wait_ge(pool_step, n)
            n = step(pool.affine_select(out=head_mask[:, :, :], in_=head_mask[:, :, :], compare_op=ALU.is_ge,
                                        fill=0.0, base=HD - 1, pattern=[[HD, HEADS], [0, HD]],
                                        channel_multiplier=-1))
            pool.wait_ge(pool_step, n)
            pool.drain().then_inc(const_late, 1)
            rstd_of(3)
            rstd_of(4)

            one = ones[:, 0:256]

            def split_pair(i):
                for odd in range(2):
                    e = 2 * i + odd
                    for w2, (free, done) in enumerate(((z_ready, w1_split), (y_done, w2_split))):
                        pool.wait_ge(free, CREDIT + 4 * e - 4)
                        cols = 256 * w2
                        raw = wexp[:, bass.ds(e * 512 + cols, 256)]
                        hi, lo = w_hi[odd][:, cols:cols + 256], w_lo[odd][:, cols:cols + 256]
                        pool.tensor_tensor(hi, raw, one, ALU.mult)
                        pool.drain()
                        pool.tensor_tensor(lo, raw, hi.bitcast(f32), ALU.subtract).then_inc(done, 1)

            pool.wait_ge(exp_in, 16)
            with pool.Fori(0, EXPERTS // 2) as i:
                split_pair(i)

            pool.wait_ge(wb_scale, 1)
            blocks = wq4[:, :, :].rearrange("p c (b k) -> p (c b) k", k=QBLOCK)
            shape = [128, 3 * IC * NBLK, QBLOCK]
            ints = wb_i[:, :, :].rearrange("p c (b k) -> p (c b) k", k=QBLOCK)
            deq = wb_d[:, :, :].rearrange("p c (b k) -> p (c b) k", k=QBLOCK)
            n = step(pool.tensor_tensor(ints, blocks, wb_r[:, :].unsqueeze(2).broadcast_to(shape), ALU.mult))
            pool.wait_ge(pool_step, n)
            n = step(pool.tensor_scalar(wb_i[:, :, :], wb_i[:, :, :], ROUND, -ROUND, ALU.add, ALU.add))
            pool.wait_ge(pool_step, n)
            pool.tensor_tensor(deq, ints, wb_s[:, :].unsqueeze(2).broadcast_to(shape), ALU.mult)\
                .then_inc(wb_ready, 1)
            pool.wait_ge(kv_raw_ready, 1)
            for b in range(BATCH):
                pool.tensor_tensor(kv[:, b, :], kv_raw[:, b, :],
                                   head_mask[:, :, :].rearrange("p a b -> p (a b)"), ALU.mult)
            pool.tensor_tensor(kc[:, :, :], ksum[:, :].unsqueeze(2).broadcast_to([128, BATCH, HEADS]),
                               head_mask[:, :, 0].unsqueeze(1).broadcast_to([128, BATCH, HEADS]), ALU.mult)\
                .then_inc(kv_ready, 1)
            rstd_of(5)
            rstd_of(6)
            for c in range(IC):
                pool.wait_ge(wT_ready, c + 1)
                k = slice(IC * c, IC * c + IC)
                pool.tensor_tensor(wT_lo[:, k, :], wT[:, k, :], wT_hi[:, k, :].bitcast(f32), ALU.subtract)\
                    .then_inc(wT_split, 1)
            rstd_of(7)
            rstd_of(8)
            for k in STG:
                pool.wait_ge(amax_ready[k], 1)
                pool.partition_all_reduce(gmax[k][:, :], amax1[k][:, :], 128, bass.bass_isa.ReduceOp.absmax)\
                    .then_inc(gmax_ready[k], 1)

        @block.scalar
        def _(act):
            steps = [0]
            act.sem_inc(gelu_done, CREDIT)
            act.sem_inc(hi_done, CREDIT)

            def evac(dst, src, ready, n, done):
                act.wait_ge(ready, n)
                act.activation(dst, src, ACT.Copy).then_inc(done, 1)

            act.dma_start(row[:, :], rows).then_inc(row_in, 16)
            act.wait_ge(g_mm, 1)
            act.activation(tg[:, :], bank[2][:, 0:4], ACT.Tanh).then_inc(tg_ready, 1)
            act.wait_ge(kT_mm, 1)
            act.activation(kT[:, :], bank[0][:, 0:256], ACT.Identity, bias=A("bk", 1)).then_inc(kT_ready, 1)
            evac(v0[:, :, :].rearrange("p b d -> p (b d)"), bank[3][0:CTX, :], v0_mm, 1, v0_ready)
            act.wait_ge(wqk_mm, 1)
            act.activation(wqk[:, :], bank[1][:, 0:256], ACT.Copy)
            act.activation(bqk[:, :], bank[0][0:1, 0:256], ACT.Copy).then_inc(wqk_ready, 1)
            evac(xT[:, 0:HT], bank[6][:, :], xT_mm, 1, xT_ready)
            evac(k1[:, :, :].rearrange("p b d -> p (b d)"), bank[4][0:CTX, :], kv1_mm, 1, k1_ready)
            evac(v1[:, :, :].rearrange("p b d -> p (b d)"), bank[5][0:CTX, :], kv1_mm, 2, v1_ready)
            evac(xT[:, HT:], bank[7][:, :], xT_mm, 2, xT_ready)
            act.wait_ge(k1_soft, 1)
            act.activation(k1e[:, :, :], k1[:, :, :], ACT.Exp).then_inc(k1_soft, 1)
            for h in range(HALVES):
                act.wait_ge(s_sub, h + 1)
                if h >= 1:
                    act.wait_ge(prT_mm, h)
                act.activation(pr[:, :, :], sc[:, :, :], ACT.Exp).then_inc(pr_ready, 1)
                if h >= 1:
                    act.wait_ge(pv_mm, h)
                evac(prT[:, :], bank[2 + h][0:CTX, :], prT_mm, h + 1, prT_ready)
            for h in range(HALVES):
                evac(half(xhi, h), bank[6 + h][:, :], xT_mm, 3 + h, xhi_ready)
            for h in range(HALVES):
                act.wait_ge(dm_ready, h + 1)
                act.activation(ex[:, :], m2[:, :], ACT.Exp).then_inc(ex_ready, 1)
            act.activation(warm[:, 0:1], row[0:1, 0:1], ACT.Gelu).then_inc(act_step, 1)
            for h in range(HALVES):
                evac(half(gateT, h), bank[2 + h][:, 0:256].bitcast(bf16), gateT_mm, h + 1, gateT_ready)

            def gelu(u, j):
                act.wait_ge(z_ready, CREDIT + u + 1)
                act.wait_ge(gated, CREDIT + u - NB + 1)
                act.activation(ge[j % NB][:, :], bank[4 + j % NB][:, :], ACT.Gelu).then_inc(gelu_done, 1)

            def high(u, j):
                act.wait_ge(gated, CREDIT + u + 1)
                act.wait_ge(y_done, CREDIT + u - NB + 1)
                act.activation(h_hi[j % NB][:, :], hm[j % NB][:, :], ACT.Copy).then_inc(hi_done, 1)

            def units(i, last):
                for j in range(8):
                    if not (last and j == 7):
                        gelu(8 * i + j + 1, j + 1)
                    high(8 * i + j, j)

            gelu(0, 0)
            with act.Fori(0, EXPERTS // 2 - 1) as i:
                units(i, False)
            units(EXPERTS // 2 - 1, True)

            for h in range(HALVES):
                evac(half(yT, h), bank[h][:, :], y_done, CREDIT + 30 + 2 * h, yT_ready)
            act.activation(warm[:, 1:2], row[0:1, 0:1], ACT.Exp).then_inc(act_step, 1)
            act.wait_ge(kv_mm, 1)
            act.activation(kv_raw[:, :, :].rearrange("p b d -> p (b d)"), bank[2][:, :], ACT.Copy)
            act.activation(ksum[:, :], bank[3][:, 0:BATCH], ACT.Copy).then_inc(kv_raw_ready, 1)
            for c in range(IC):
                act.wait_ge(wT_mm, c + 1)
                src = bank[2 + c % 2][:, 0:IC * D].rearrange("p (c d) -> p c d", d=D)
                k = slice(IC * c, IC * c + IC)
                act.activation(wT_hi[:, k, :], src, ACT.Copy)
                act.activation(wT[:, k, :], src, ACT.Copy).then_inc(wT_ready, 1)
            for h in range(HALVES):
                evac(half(xT, h), bank[6 + h][:, :], xT_mm, 5 + h, xT_ready)
                act.wait_ge(q_sub, h + 1)
                if h >= 1:
                    act.wait_ge(qn_ready, h)
                act.activation(qe[:, :], qs[:, :], ACT.Exp).then_inc(qe_ready, 1)
                if h >= 1:
                    act.wait_ge(nd_mm, h)
                evac(qeT[:, :], bank[2][:, :], qeT_mm, h + 1, qeT_ready)
                if h >= 1:
                    act.wait_ge(proj_mm, h)
                evac(aoT[:, :], bank[3][:, :], aoT_mm, h + 1, aoT_ready)
            act.activation(warm[:, 0:1], row[0:1, 0:1], ACT.Sigmoid).then_inc(act_step, 1)
            for h in range(HALVES):
                evac(half(x4T, h), bank[4 + h][:, :], x4T_mm, h + 1, x4T_ready)
            for n in range(2 * IC * HALVES):
                c, h = n // HALVES, n % HALVES
                dst = gq if c < IC else up
                act.wait_ge(gu_mm, n + 1)
                act.activation(half(dst[:, c % IC, :], h), bank[n % 6][:, :], ACT.Copy).then_inc(gu_ready, 1)
            act.wait_ge(mul_ready["g"], 1)
            for c in range(IC):
                act.activation(ng[:, c, :], gq[:, c, :], ACT.Copy, scale=mul["g"][:, :]).then_inc(ng_ready, 1)
                act.wait_ge(ng_ready, c + 1)
                act.activation(sg[:, c, :], ng[:, c, :], ACT.Sigmoid, scale=scale["g"][:, :])\
                    .then_inc(sg_ready, 1)
            act.wait_ge(mul_ready["u"], 1)
            for c in range(IC):
                act.activation(nu[:, c, :], up[:, c, :], ACT.Copy, scale=mul["u"][:, :]).then_inc(nu_ready, 1)
            act.wait_ge(mul_ready["o"], 1)
            for c in range(IC):
                act.activation(n4[:, c, :], og[:, c, :], ACT.Copy, scale=mul["o"][:, :]).then_inc(n4_ready, 1)

        @block.vector
        def _(dve):
            steps = [0]

            def step(ins):
                steps[0] += 1
                ins.then_inc(dve_step, 1)
                return steps[0]

            def link(ins):
                dve.wait_ge(dve_step, step(ins))

            dve.sem_inc(gated, CREDIT)
            dve.sem_inc(lo_done, CREDIT)
            norms = [0]

            def layernorm(src, h):
                norms[0] += 1
                n = norms[0]
                for t in range(TILES):
                    m = step(dve.bn_stats(stats[:, t, :], src[:, h * TILES + t, :]))
                dve.wait_ge(dve_step, m)
                for t in range(TILES):
                    m = step(dve.bn_aggr(mv[:, t, :], stats[:, t, :]))
                dve.wait_ge(dve_step, m)
                dve.tensor_scalar(var[:, :], mv[:, :, 1], LN_EPS, None, ALU.add).then_inc(var_ready, 1)
                if n > 2:
                    dve.wait_ge(xT_mm, n - 2)
                dve.wait_ge(rstd_ready, n)
                for t in range(TILES):
                    last = dve.tensor_scalar(xn[:, h * TILES + t, :], src[:, h * TILES + t, :],
                                             mv[:, t, 0:1], rstd[:, t:t + 1], ALU.subtract, ALU.mult)
                last.then_inc(xn_ready, 1)

            def weight_scales():
                dve.wait_ge(lpbq_in, 16)
                link(dve.tensor_reduce(wb_max[:, :], wq4[:, :, :].rearrange("p c (b k) -> p (c b) k", k=QBLOCK),
                                       X, ALU.max, apply_absolute_value=True))
                link(dve.tensor_scalar(wb_s[:, :], wb_max[:, :], 1.0 / WQMAX, QMIN_SCALE, ALU.mult, ALU.max))
                dve.reciprocal(wb_r[:, :], wb_s[:, :]).then_inc(wb_scale, 1)

            def scores(h):
                s = bank[h][:, 0:TILES * CTX].rearrange("p (t c) -> p t c", c=CTX)
                dve.wait_ge(s_mm, h + 1)
                link(dve.tensor_reduce(smax[:, :], s, X, ALU.max))
                if h >= 1:
                    dve.wait_ge(pr_ready, h)
                dve.tensor_tensor(sc[:, :, :], s, smax[:, :].unsqueeze(2).broadcast_to([128, TILES, CTX]),
                                  ALU.subtract).then_inc(s_sub, 1)
                dve.wait_ge(pr_ready, h + 1)
                link(dve.tensor_reduce(ssum[:, :], pr[:, :, :], X, ALU.add))
                link(dve.reciprocal(smax[:, :], ssum[:, :]))
                dve.wait_ge(tg_ready, 1)
                link(dve.tensor_scalar(ssum[:, :], smax[:, :], tg[:, G_XATTN0:G_XATTN0 + 1], None, ALU.mult))

            def add_attention(h):
                dve.wait_ge(pv_mm, h + 1)
                for t in range(TILES):
                    last = dve.scalar_tensor_tensor(out=x2[:, h * TILES + t, :], in0=bank[4 + h][:, t * D:t * D + D],
                                                    scalar=ssum[:, t:t + 1], in1=xin[:, h * TILES + t, :],
                                                    op0=ALU.mult, op1=ALU.add)
                link(last)

            def route(h):
                wide = [128, TILES, EXPERTS]

                def over(t):
                    return t[:, :].unsqueeze(2).broadcast_to(wide)

                order = rank[:, :].unsqueeze(1).broadcast_to(wide)

                def first_of(vals, top, onehot):
                    link(dve.tensor_reduce(top[:, :], vals[:, :, :], X, ALU.max))
                    link(dve.tensor_tensor(eq[:, :, :], vals[:, :, :], over(top), ALU.is_equal))
                    link(dve.tensor_tensor(eq[:, :, :], eq[:, :, :], order, ALU.mult))
                    link(dve.tensor_reduce(mr[:, :], eq[:, :, :], X, ALU.max))
                    link(dve.tensor_tensor(onehot[:, :, :], order, over(mr), ALU.is_equal))

                dve.wait_ge(lg_mm, h + 1)
                dve.tensor_copy(lg[:, :, :], bank[h][:, 0:TILES * EXPERTS].rearrange("p (t e) -> p t e", e=EXPERTS))\
                    .then_inc(lg_read, 1)
                dve.wait_ge(lg_read, h + 1)
                first_of(lg, m1, top1)
                link(dve.scalar_tensor_tensor(out=lg2[:, :, :], in0=top1[:, :, :], scalar=-3.0e38,
                                              in1=lg[:, :, :], op0=ALU.mult, op1=ALU.add))
                first_of(lg2, m2, top2)
                dve.tensor_tensor(m2[:, :], m2[:, :], m1[:, :], ALU.subtract).then_inc(dm_ready, 1)
                dve.wait_ge(ex_ready, h + 1)
                link(dve.tensor_scalar(mr[:, :], ex[:, :], 1.0, None, ALU.add))
                link(dve.reciprocal(m1[:, :], mr[:, :]))
                link(dve.tensor_tensor(m2[:, :], m1[:, :], ex[:, :], ALU.mult))
                dve.tensor_tensor(top1[:, :, :], top1[:, :, :], over(m1), ALU.mult)
                link(dve.tensor_tensor(top2[:, :, :], top2[:, :, :], over(m2), ALU.mult))
                link(dve.tensor_tensor(gate[:, :, :], top1[:, :, :], top2[:, :, :], ALU.add))
                part = [tiles(gpart, h)[:, :, EXPERTS * k:EXPERTS * (k + 1)] for k in range(3)]
                link(dve.tensor_copy(part[0], gate[:, :, :]))
                link(dve.tensor_tensor(rest[:, :, :], gate[:, :, :], part[0], ALU.subtract))
                link(dve.tensor_copy(part[1], rest[:, :, :]))
                link(dve.tensor_tensor(lg2[:, :, :], rest[:, :, :], part[1], ALU.subtract))
                dve.tensor_copy(part[2], lg2[:, :, :]).then_inc(gpart_ready, 1)

            for h in range(HALVES):
                dve.wait_ge(x_in[h], 16)
                layernorm(xin, h)
            dve.wait_ge(pa_in, 16)
            link(dve.tensor_copy(rw_hi[:, :], A("rwT", EXPERTS)))
            dve.tensor_tensor(rw_lo[:, :], A("rwT", EXPERTS), rw_hi[:, :].bitcast(f32), ALU.subtract)\
                .then_inc(rw_ready, 1)
            dve.wait_ge(k1_ready, 1)
            k1h = k1[:, :, :].rearrange("p b (a c) -> p (b a) c", c=HD)
            k1eh = k1e[:, :, :].rearrange("p b (a c) -> p (b a) c", c=HD)
            kwide = [CTX, BATCH * HEADS, HD]
            link(dve.tensor_reduce(k1max[:, :], k1h, X, ALU.max))
            dve.tensor_tensor(k1h, k1h, k1max[:, :].unsqueeze(2).broadcast_to(kwide), ALU.subtract)\
                .then_inc(k1_soft, 1)
            for h in range(HALVES):
                scores(h)
                add_attention(h)
                layernorm(x2, h)
            for h in range(HALVES):
                dve.wait_ge(xhi_ready, h + 1)
                dve.tensor_tensor(half(xlo, h), bank[6 + h][:, :], half(xhi, h).bitcast(f32), ALU.subtract)\
                    .then_inc(xlo_ready, 1)
            dve.wait_ge(const_late, 1)
            for h in range(HALVES):
                route(h)
            dve.wait_ge(k1_soft, 2)
            link(dve.tensor_reduce(k1sum[:, :], k1eh, X, ALU.add))
            link(dve.reciprocal(k1max[:, :], k1sum[:, :]))
            dve.tensor_tensor(k1h, k1eh, k1max[:, :].unsqueeze(2).broadcast_to(kwide), ALU.mult)\
                .then_inc(k1_soft, 1)
            weight_scales()

            def low(u, j):
                dve.wait_ge(hi_done, CREDIT + u + 1)
                dve.wait_ge(y_done, CREDIT + u - NB + 1)
                dve.tensor_tensor(h_lo[j % NB][:, :], hm[j % NB][:, :], h_hi[j % NB][:, :].bitcast(f32),
                                  ALU.subtract).then_inc(lo_done, 1)

            def units(i, last):
                for j in range(8):
                    if not (last and j == 7):
                        gate_unit(i, j + 1)
                    low(8 * i + j, j)

            def gate_unit(i, j):
                u = 8 * i + j
                dve.wait_ge(gelu_done, CREDIT + u + 1)
                if j % FC == 0:
                    dve.wait_ge(gb_ready, 4 * i + j // FC + 1)
                dve.wait_ge(hi_done, CREDIT + u - NB + 1)
                dve.tensor_tensor(hm[j % NB][:, :], ge[j % NB][:, :], bank[2 + (j // FC) % 2][:, :], ALU.mult)\
                    .then_inc(gated, 1)

            gate_unit(0, 0)
            with dve.Fori(0, EXPERTS // 2 - 1) as i:
                units(i, False)
            units(EXPERTS // 2 - 1, True)

            def linear_attention(h):
                heads = TILES * HEADS
                wide = [128, heads, HD]

                def by_head(t):
                    return t[:, :].rearrange("p (a c) -> p a c", c=HD)

                def over(t):
                    return t[:, :].unsqueeze(2).broadcast_to(wide)

                dve.wait_ge(q_mm, h + 1)
                link(dve.tensor_reduce(qmax[:, :], by_head(bank[0]), X, ALU.max))
                if h >= 1:
                    dve.wait_ge(qe_ready, h)
                dve.tensor_tensor(by_head(qs), by_head(bank[0]), over(qmax), ALU.subtract).then_inc(q_sub, 1)
                dve.wait_ge(qe_ready, h + 1)
                link(dve.tensor_reduce(qsum[:, :], by_head(qe), X, ALU.add))
                link(dve.reciprocal(qmax[:, :], qsum[:, :]))
                dve.tensor_tensor(by_head(qn), by_head(qe), over(qmax), ALU.mult).then_inc(qn_ready, 1)
                dve.wait_ge(nd_mm, h + 1)
                link(dve.reciprocal(dinv[:, :], bank[5][:, 0:heads]))
                link(dve.tensor_tensor(by_head(att), by_head(bank[4]), over(dinv), ALU.mult))
                if h >= 1:
                    dve.wait_ge(aoT_mm, h)
                dve.tensor_tensor(ao[:, :], att[:, :], qn[:, :], ALU.add).then_inc(ao_ready, 1)
                dve.wait_ge(proj_mm, h + 1)
                dve.scalar_tensor_tensor(out=tiles(x4, h).rearrange("p t d -> p (t d)"), in0=bank[1][:, :],
                                         scalar=tg[:, G_XATTN1:G_XATTN1 + 1],
                                         in1=tiles(x3, h).rearrange("p t d -> p (t d)"),
                                         op0=ALU.mult, op1=ALU.add).then_inc(x4_ready, 1)
                dve.wait_ge(x4_ready, h + 1)

            for h in range(HALVES):
                dve.wait_ge(yN_mm, h + 1)
                dve.scalar_tensor_tensor(out=tiles(x3, h).rearrange("p t d -> p (t d)"), in0=bank[4 + h][:, :],
                                         scalar=tg[:, G_FFN0:G_FFN0 + 1],
                                         in1=tiles(x2, h).rearrange("p t d -> p (t d)"),
                                         op0=ALU.mult, op1=ALU.add).then_inc(x3_ready, 1)
                dve.wait_ge(x3_ready, h + 1)
                layernorm(x3, h)
            for h in range(HALVES):
                linear_attention(h)
                layernorm(x4, h)
                dve.wait_ge(xn_ready, 7 + h)
                step(dve.tensor_reduce(amax["x"][:, h:h + 1], tiles(xn, h).rearrange("p t d -> p (t d)"),
                                       X, ALU.max, apply_absolute_value=True))

            def max_over(k, n):
                dve.wait_ge(dve_step, steps[0])
                dve.tensor_reduce(amax1[k][:, :], amax[k][:, 0:n], X, ALU.max).then_inc(amax_ready[k], 1)

            def make_scale(k):
                dve.wait_ge(gmax_ready[k], 1)
                if k == "x":
                    link(dve.tensor_scalar(scale[k][:, :], gmax[k][:, :], 1.0 / QMAX, QMIN_SCALE,
                                           ALU.mult, ALU.max))
                    dve.reciprocal(mul[k][:, :], scale[k][:, :]).then_inc(mul_ready[k], 1)
                    return
                link(dve.tensor_scalar(scale[k][:, :], gmax[k][:, :], unitq[k][:, :], QMIN_SCALE,
                                       ALU.mult, ALU.max))
                link(dve.reciprocal(rcp[k][:, :], scale[k][:, :]))
                dve.tensor_tensor(mul[k][:, :], rcp[k][:, :], unit[k][:, :], ALU.mult).then_inc(mul_ready[k], 1)

            def make_unit(k, a, b):
                link(dve.tensor_scalar(unit[k][:, :], a, b, None, ALU.mult))
                link(dve.tensor_scalar(unitq[k][:, :], unit[k][:, :], 1.0 / QMAX, None, ALU.mult))

            max_over("x", HALVES)
            make_scale("x")
            dve.wait_ge(mul_ready["x"], 1)
            dve.wait_ge(xT_mm, 8)
            for h in range(HALVES):
                link(dve.tensor_scalar(half(nx, h), bank[6 + h][:, :], mul["x"][:, :], None, ALU.mult))
                link(dve.tensor_copy(half(xhi, h), half(nx, h)))
                dve.tensor_tensor(half(xlo, h), half(nx, h), half(xhi, h).bitcast(f32), ALU.subtract)\
                    .then_inc(nx_ready, 1)
            for k in ("g", "u"):
                make_unit(k, scale["x"][:, :], 1.0)
            for k, t, base in (("g", gq, 0), ("u", up, IC * HALVES)):
                for n in range(IC * HALVES):
                    dve.wait_ge(gu_ready, base + n + 1)
                    step(dve.tensor_reduce(amax[k][:, n:n + 1], half(t[:, n // HALVES, :], n % HALVES),
                                           X, ALU.max, apply_absolute_value=True))
                max_over(k, IC * HALVES)
                if k == "u":
                    continue
                make_scale(k)
            make_scale("u")
            make_unit("p", scale["g"][:, :], 1.0 / SIG_STEPS)
            for c in range(IC):
                dve.wait_ge(sg_ready, c + 1)
                link(dve.tensor_scalar(sq[:, c, :], sg[:, c, :], SIG_STEPS, None, ALU.mult))
                link(dve.tensor_tensor(pg[:, c, :], ng[:, c, :], sq[:, c, :], ALU.mult))
                step(dve.tensor_reduce(amax["p"][:, c:c + 1], pg[:, c, :], X, ALU.max,
                                       apply_absolute_value=True))
            max_over("p", IC)
            make_scale("p")
            make_unit("o", scale["p"][:, :], scale["u"][:, :])
            for c in range(IC):
                link(dve.tensor_scalar(n3[:, c, :], pg[:, c, :], mul["p"][:, :], None, ALU.mult))
                dve.wait_ge(nu_ready, c + 1)
                link(dve.tensor_tensor(og[:, c, :], n3[:, c, :], nu[:, c, :], ALU.mult))
                step(dve.tensor_reduce(amax["o"][:, c:c + 1], og[:, c, :], X, ALU.max,
                                       apply_absolute_value=True))
            max_over("o", IC)
            make_scale("o")
            link(dve.tensor_scalar(tscale[:, :], scale["o"][:, :], tg[:, G_FFN1:G_FFN1 + 1], None, ALU.mult))
            for c in range(IC):
                dve.wait_ge(n4_ready, c + 1)
                link(dve.tensor_copy(o_hi[:, c, :], n4[:, c, :]))
                dve.tensor_tensor(o_lo[:, c, :], n4[:, c, :], o_hi[:, c, :].bitcast(f32), ALU.subtract)\
                    .then_inc(olo_ready, 1)
            dve.wait_ge(x4T_ready, HALVES)
            for h in range(HALVES):
                dve.wait_ge(dn_mm, h + 1)
                dve.scalar_tensor_tensor(out=half(res, h), in0=bank[6 + h][:, :], scalar=tscale[:, :],
                                         in1=half(x4T, h), op0=ALU.mult, op1=ALU.add).then_inc(res_ready, 1)

        @block.tensor
        def _(pe):
            pe.sem_inc(z_ready, CREDIT)
            pe.sem_inc(y_done, CREDIT)
            mm = pe.matmul

            def transposes(dst, src, h, ident_=ident):
                for t in range(TILES):
                    last = pe.transpose(dst[:, t * 128:(t + 1) * 128], src[:, h * TILES + t, :], ident_[:, :])
                return last

            def three(dst, whi, wlo, xh, xl, start, stop):
                mm(dst, whi, xh, start=start, stop=False)
                mm(dst, whi, xl, start=False, stop=False)
                return mm(dst, wlo, xh, start=False, stop=stop)

            pe.wait_ge(const_ready, 1)
            pe.wait_ge(row_in, 16)
            mm(bank[2][:, 0:4], ones[0:1, 0:128], R("g", 4), start=True, stop=True).then_inc(g_mm, 1)
            pe.wait_ge(pa_in, 16)
            mm(bank[0][:, 0:256], A("wkT", D), A("ctxT", 256), start=True, stop=True).then_inc(kT_mm, 1)

            def context_rows(dst, w, bias):
                mm(dst, ones[0:1, 0:CTX], bias.unsqueeze(1).broadcast_to([1, BATCH, D]), start=True, stop=False)
                for b in range(BATCH):
                    last = mm(dst[:, b * D:(b + 1) * D], A("ctxT", 256)[:, b * CTX:(b + 1) * CTX], w,
                              start=False, stop=(b == BATCH - 1))
                return last

            context_rows(bank[3][0:CTX, :], A("wvT", D), R("bv0")).then_inc(v0_mm, 1)
            pe.wait_ge(kT_ready, 1)
            mm(bank[1][:, 0:256], A("wq", D), kT[:, :], start=True, stop=True)
            mm(bank[0][0:1, 0:256], A("bq", 1), kT[:, :], start=True, stop=True).then_inc(wqk_mm, 1)
            pe.wait_ge(xn_ready, 1)
            transposes(bank[6], xn, 0).then_inc(xT_mm, 1)
            pe.wait_ge(pb_in, 16)
            context_rows(bank[4][0:CTX, :], B("wkT"), R("bk1")).then_inc(kv1_mm, 1)
            context_rows(bank[5][0:CTX, :], B("wvT"), R("bv1")).then_inc(kv1_mm, 1)
            pe.wait_ge(xn_ready, 2)
            transposes(bank[7], xn, 1).then_inc(xT_mm, 1)
            pe.wait_ge(wqk_ready, 1)

            def score_products(h):
                pe.wait_ge(xT_ready, h + 1)
                bias = bqk[0:1, h * BPH * CTX:(h + 1) * BPH * CTX].rearrange("p (b c) -> p b c", c=CTX)
                s = bank[h][:, 0:TILES * CTX]
                mm(s, ones[0:1, 0:128], bias.unsqueeze(2).broadcast_to([1, BPH, TPB, CTX]), start=True, stop=False)
                for t in range(TILES):
                    b = h * BPH + t // TPB
                    last = mm(s[:, t * CTX:(t + 1) * CTX], half(xT, h)[:, t * D:(t + 1) * D],
                              wqk[:, b * CTX:(b + 1) * CTX], start=False, stop=(t == TILES - 1))
                last.then_inc(s_mm, 1)

            def attend(h):
                pe.wait_ge(pr_ready, h + 1)
                for t in range(TILES):
                    last = pe.transpose(bank[2 + h][0:CTX, t * D:(t + 1) * D], pr[:, t, :], ident[:, :])
                last.then_inc(prT_mm, 1)
                pe.wait_ge(prT_ready, h + 1)
                for t in range(TILES):
                    last = mm(bank[4 + h][:, t * D:(t + 1) * D], prT[:, t * D:(t + 1) * D],
                              v0[:, h * BPH + t // TPB, :], start=True, stop=True)
                last.then_inc(pv_mm, 1)

            score_products(0)
            score_products(1)
            pe.wait_ge(v0_ready, 1)
            attend(0)
            pe.wait_ge(v1_ready, 1)
            attend(1)
            for h in range(HALVES):
                pe.wait_ge(xn_ready, 3 + h)
                transposes(bank[6 + h], xn, h).then_inc(xT_mm, 1)
            pe.wait_ge(rw_ready, 1)
            for h in range(HALVES):
                pe.wait_ge(xlo_ready, h + 1)
                for t in range(TILES):
                    k = slice(h * HT + t * D, h * HT + (t + 1) * D)
                    last = three(bank[h][:, t * EXPERTS:(t + 1) * EXPERTS], xhi[:, k], xlo[:, k],
                                 rw_hi[:, :], rw_lo[:, :], True, True)
                last.then_inc(lg_mm, 1)

            def z_unit(u, j, e):
                odd, h, c = (j // 4) % 2, (j // 2) % 2, j % 2
                if j % 4 == 0:
                    pe.wait_ge(w1_split, e + 1)
                pe.wait_ge(gelu_done, CREDIT + u - NB + 1)
                k = slice(c * D, (c + 1) * D)
                three(bank[4 + j % NB][:, :], w_hi[odd][:, k], w_lo[odd][:, k], half(xhi, h), half(xlo, h),
                      True, True).then_inc(z_ready, 1)

            def gate_rows(k, e, h):
                pe.wait_ge(gated, CREDIT + FC * k - 2)
                lhsT = sel[:, :, :].rearrange("p e m -> p (e m)")[:, bass.ds(e * 128, 128)]
                mm(bank[2 + h][:, :], lhsT, half(gateT, h), start=True, stop=True).then_inc(gb_ready, 1)

            def y_unit(u, j, e, last):
                odd, h, c = (j // 4) % 2, (j // 2) % 2, j % 2
                if j % 4 == 0:
                    pe.wait_ge(w2_split, e + 1)
                pe.wait_ge(lo_done, CREDIT + u + 1)
                k = slice(256 + c * D, 256 + (c + 1) * D)
                b = j % NB
                three(bank[h][:, :], w_hi[odd][:, k], w_lo[odd][:, k], h_hi[b][:, :], h_lo[b][:, :],
                      False, last and j // 4 == 1 and c == 1).then_inc(y_done, 1)

            def units(i, last):
                for j in range(8):
                    if j % 2 == 0 and not (last and j == 6):
                        k = j // 2 + 1
                        gate_rows(4 * i + k, 2 * i + k // 2, k % 2)
                    if not (last and j >= 5):
                        z_unit(8 * i + j + 3, j + 3, 2 * i + (j + 3) // 4)
                    y_unit(8 * i + j, j, 2 * i + j // 4, last)

            for u in range(3):
                z_unit(u, u, 0)
            pe.wait_ge(lg_read, HALVES)
            for h in range(HALVES):
                mm(bank[h][:, :], zerob[:, 0:128], zerob[:, :], start=True, stop=False)
            for h in range(HALVES):
                pe.wait_ge(gpart_ready, h + 1)
                transposes(bank[2 + h][:, 0:256].bitcast(bf16), gpart, h, identb).then_inc(gateT_mm, 1)
            pe.wait_ge(gateT_ready, HALVES)
            gate_rows(0, 0, 0)
            with pe.Fori(0, EXPERTS // 2 - 1) as i:
                units(i, False)
            units(EXPERTS // 2 - 1, True)

            pe.wait_ge(k1_soft, 3)
            for b in range(BATCH):
                mm(bank[2][:, b * D:(b + 1) * D], k1[:, b, :], v1[:, b, :], start=True, stop=True)
            for b in range(BATCH):
                last = mm(bank[3][:, b:b + 1], k1[:, b, :], ones[0:CTX, 0:1], start=True, stop=True)
            last.then_inc(kv_mm, 1)
            for h in range(HALVES):
                pe.wait_ge(yT_ready, h + 1)
                for t in range(TILES):
                    last = pe.transpose(bank[4 + h][:, t * D:(t + 1) * D], half(yT, h)[:, t * D:(t + 1) * D],
                                        ident[:, :])
                last.then_inc(yN_mm, 1)
            pe.wait_ge(wb_ready, 1)
            pe.wait_ge(kv_raw_ready, 1)
            for c in range(IC):
                if c >= 2:
                    pe.wait_ge(wT_ready, c - 1)
                for k in range(IC):
                    last = pe.transpose(bank[2 + c % 2][:, k * D:(k + 1) * D], wb_d[:, IC * c + k, :], ident[:, :])
                last.then_inc(wT_mm, 1)
            for h in range(HALVES):
                pe.wait_ge(xn_ready, 5 + h)
                transposes(bank[6 + h], xn, h).then_inc(xT_mm, 1)
            pe.wait_ge(wT_ready, IC)

            for h in range(HALVES):
                pe.wait_ge(xT_ready, 3 + h)
                if h >= 1:
                    pe.wait_ge(q_sub, h)
                mm(bank[0][:, :], ones[0:1, 0:128], R("bq1").unsqueeze(1).broadcast_to([1, TILES, D]),
                   start=True, stop=False)
                for t in range(TILES):
                    last = mm(bank[0][:, t * D:(t + 1) * D], half(xT, h)[:, t * D:(t + 1) * D], B("wqT"),
                              start=False, stop=(t == TILES - 1))
                last.then_inc(q_mm, 1)
                pe.wait_ge(qe_ready, h + 1)
                for t in range(TILES):
                    last = pe.transpose(bank[2][:, t * D:(t + 1) * D], qe[:, t * D:(t + 1) * D], ident[:, :])
                last.then_inc(qeT_mm, 1)
                pe.wait_ge(qeT_ready, h + 1)
                if h == 0:
                    pe.wait_ge(kv_ready, 1)
                    pe.wait_ge(x3_ready, HALVES)
                else:
                    pe.wait_ge(ao_ready, h)
                for t in range(TILES):
                    b = h * BPH + t // TPB
                    q = qeT[:, t * D:(t + 1) * D]
                    mm(bank[4][:, t * D:(t + 1) * D], q, kv[:, b, :], start=True, stop=True)
                    last = mm(bank[5][:, t * HEADS:(t + 1) * HEADS], q, kc[:, b, :], start=True, stop=True)
                last.then_inc(nd_mm, 1)
                pe.wait_ge(ao_ready, h + 1)
                for t in range(TILES):
                    last = pe.transpose(bank[3][:, t * D:(t + 1) * D], ao[:, t * D:(t + 1) * D], ident[:, :])
                last.then_inc(aoT_mm, 1)
                pe.wait_ge(aoT_ready, h + 1)
                if h >= 1:
                    pe.wait_ge(x4_ready, h)
                mm(bank[1][:, :], ones[0:1, 0:128], R("bp1").unsqueeze(1).broadcast_to([1, TILES, D]),
                   start=True, stop=False)
                for t in range(TILES):
                    last = mm(bank[1][:, t * D:(t + 1) * D], aoT[:, t * D:(t + 1) * D], B("wpT"),
                              start=False, stop=(t == TILES - 1))
                last.then_inc(proj_mm, 1)
            for h in range(HALVES):
                pe.wait_ge(x4_ready, h + 1)
                transposes(bank[4 + h], x4, h).then_inc(x4T_mm, 1)
                pe.wait_ge(xn_ready, 7 + h)
                transposes(bank[6 + h], xn, h).then_inc(xT_mm, 1)

            pe.wait_ge(wT_split, IC)
            pe.wait_ge(x4T_ready, HALVES)
            for n in range(2 * IC * HALVES):
                c, h = n // HALVES, n % HALVES
                w = c + IC if c < IC else c - IC
                if n < HALVES:
                    pe.wait_ge(nx_ready, h + 1)
                if n >= 6:
                    pe.wait_ge(gu_ready, n - 5)
                three(bank[n % 6][:, :], wT_hi[:, w, :], wT_lo[:, w, :], half(xhi, h), half(xlo, h),
                      True, True).then_inc(gu_mm, 1)
            for c in range(IC):
                pe.wait_ge(olo_ready, c + 1)
                for h in range(HALVES):
                    last = three(bank[6 + h][:, :], wT_hi[:, 2 * IC + c, :], wT_lo[:, 2 * IC + c, :],
                                 half(o_hi[:, c, :], h), half(o_lo[:, c, :], h), c == 0, c == IC - 1)
                    if c == IC - 1:
                        last.then_inc(dn_mm, 1)


def kernel(**inputs):
    import concourse.bacc as _bacc
    from concourse import mybir as _mybir
    from concourse.bass_utils import run_bass_kernel_spmd as _run

    a = {k: np.asarray(v) for k, v in inputs.items()}

    def chunks(w):
        return w.reshape(-1, D, w.shape[1]).transpose(1, 0, 2)

    packa = np.concatenate([a["L0_xattn_Wq"], a["L0_xattn_Wk"].T, a["L0_xattn_Wv"].T,
                            a["ctx_1024"].reshape(BATCH * CTX, D).T, a["L0_ffn_router_w"].T,
                            a["L0_xattn_bq"][:, None], a["L0_xattn_bk"][:, None]], axis=1)
    packb = np.concatenate([a[f"L1_xattn_W{k}"].T for k in "qkvp"], axis=1)
    rows = np.concatenate([a["L0_xattn_bv"], a["L1_xattn_bq"], a["L1_xattn_bk"], a["L1_xattn_bv"],
                           a["L1_xattn_bp"], a["g_xattn"], a["g_ffn"]])[None]
    w1 = a["L0_ffn_w1"].transpose(2, 0, 1)
    w2 = a["L0_ffn_w2"].transpose(2, 0, 1).reshape(FC, D, EXPERTS, D).transpose(1, 2, 0, 3)
    experts = np.concatenate([w1, w2.reshape(D, EXPERTS, FC * D)], axis=2).reshape(D, -1)
    lpbq = np.concatenate([chunks(a["L1_ffn_w_up"]), chunks(a["L1_ffn_w_gate"]),
                           a["L1_ffn_w_down"].reshape(D, IC, D)], axis=1)
    arrays = {"in_x": a["x"], "in_packa": packa, "in_packb": packb, "in_rows": rows,
              "in_experts": experts, "in_lpbq": lpbq}
    arrays = {k: np.ascontiguousarray(v) for k, v in arrays.items()}
    nc = _bacc.Bacc("TRN2", target_bir_lowering=False, num_devices=1)
    args = [nc.dram_tensor(k, v.shape, _mybir.dt.from_np(v.dtype), kind="ExternalInput").ap()
            for k, v in arrays.items()]
    out = nc.dram_tensor("out", (D, TOKENS), _mybir.dt.float32, kind="ExternalOutput").ap()
    build(nc, *args, out)
    r = _run(nc, [arrays], core_ids=[0])
    return np.ascontiguousarray(r.results[0]["out"].T).reshape(BATCH, SEQ, D)
```

```python
import numpy as np

D = 128
BATCH, SEQ, CTX = 4, 256, 64
TOKENS = BATCH * SEQ
HALVES = 2
HT = TOKENS // HALVES
TILES = HT // D
BPH = BATCH // HALVES
TPB = SEQ // D
EXPERTS = 8
FC = 2
HEADS, HD = 16, 8
INTER = 384
IC = INTER // D
QBLOCK = 32
NBLK = D // QBLOCK
LN_EPS = 1e-5
QMAX = 32767.0
WQMAX = 7.0
QMIN_SCALE = 1e-12
SIG_STEPS = 65536.0
ROUND = 1.5 * 2.0 ** 23

PA = {"wq": 0, "wkT": 128, "wvT": 256, "ctxT": 384, "rwT": 640, "bq": 648, "bk": 649}
PA_COLS = 650
PB = {"wqT": 0, "wkT": 128, "wvT": 256, "wpT": 384}
PB_COLS = 512
ROW = {"bv0": 0, "bq1": 128, "bk1": 256, "bv1": 384, "bp1": 512, "g": 640}
ROW_COLS = 644
G_XATTN0, G_XATTN1, G_FFN0, G_FFN1 = 0, 1, 2, 3


def build(nc, x, packa, packb, rows, experts, lpbq, out):
    import concourse.bass as bass
    from concourse import mybir
    from contextlib import ExitStack

    f32, f32r, bf16, f16 = mybir.dt.float32, mybir.dt.float32r, mybir.dt.bfloat16, mybir.dt.float16
    i16, u16 = mybir.dt.int16, mybir.dt.uint16
    ACT = mybir.ActivationFunctionType
    ALU = mybir.AluOpType
    X = mybir.AxisListType.X

    ctx = ExitStack()
    with ctx:
        def sb(name, shape, dt=f32):
            return ctx.enter_context(nc.sbuf_tensor(name, shape, dt))

        def sem(name):
            return ctx.enter_context(nc.semaphore(name))

        bank = [ctx.enter_context(nc.psum_tensor(f"bank{i}", [128, 512], f32)) for i in range(8)]

        xin = sb("xin", [128, 8, D])
        pa = sb("pa", [128, PA_COLS])
        pb = sb("pb", [128, PB_COLS])
        row = sb("row", [1, ROW_COLS])
        ones_r = sb("ones_r", [1, 128], f32r)
        row_hi = sb("row_hi", [1, 2, D], f32r)
        row_lo = sb("row_lo", [1, 2, D], f32r)
        wexp = sb("wexp", [128, EXPERTS * 512])
        wq4 = sb("wq4", [128, 3 * IC, D])

        def A(name, n):
            return pa[:, PA[name]:PA[name] + n]

        def B(name):
            return pb[:, PB[name]:PB[name] + D]

        def R(name, n=D):
            return row[0:1, ROW[name]:ROW[name] + n]

        ident = sb("ident", [128, 128])
        ident16 = sb("ident16", [128, 128], f16)
        ones = sb("ones", [128, 256])
        zero16 = sb("zero16", [128, 512], f16)
        head_mask = sb("head_mask", [128, HEADS, HD])
        number = sb("number", [128, EXPERTS])
        sel = sb("sel", [128, EXPERTS, 128], f16)
        neg_half = sb("neg_half", [128, TILES])

        kT = sb("kT", [128, BATCH * CTX])
        wqk = sb("wqk", [128, BATCH * CTX])
        bqk = sb("bqk", [1, BATCH * CTX])
        v0 = sb("v0", [128, HALVES, D])
        k1 = sb("k1", [128, HALVES, D])
        k1e = sb("k1e", [128, HALVES, D])
        v1 = sb("v1", [128, HALVES, D + 1])
        k1max = sb("k1max", [128, HALVES * HEADS])
        k1sum = sb("k1sum", [128, HALVES * HEADS])
        kv_raw = sb("kv_raw", [128, BPH, HALVES, D + 1])
        kv = sb("kv", [128, BATCH, D])
        kc = sb("kc", [128, BATCH, 2, HEADS])
        tg = sb("tg", [128, 4])

        stats = sb("stats", [128, HALVES, TILES, 6])
        mv = sb("mv", [128, HALVES, TILES, 2])
        var = sb("var", [128, HALVES, TILES])
        rstd = sb("rstd", [128, HALVES, TILES])
        shift = sb("shift", [128, HALVES, TILES])
        xn = sb("xn", [128, 8, D])
        xT = sb("xT", [128, TOKENS])
        xhi = sb("xhi", [128, TOKENS], f32r)
        xlo = sb("xlo", [128, TOKENS], f32r)
        smax = sb("smax", [128, HALVES, TILES])
        ssum = sb("ssum", [128, HALVES, TILES])
        sc = sb("sc", [128, HALVES, TILES, CTX])
        prT = sb("prT", [128, HALVES, TPB, D])
        x2 = sb("x2", [128, 8, D])
        rw_hi = sb("rw_hi", [128, EXPERTS], f32r)
        rw_lo = sb("rw_lo", [128, EXPERTS], f32r)
        NT = HALVES * TILES
        lg_ = sb("lg", [128, NT, EXPERTS])
        best_ = sb("best", [128, NT, EXPERTS])
        place_ = sb("place", [128, NT, EXPERTS], mybir.dt.uint32)
        top1_ = sb("top1", [128, NT, EXPERTS])
        top2_ = sb("top2", [128, NT, EXPERTS])
        gate_ = sb("gate", [128, NT, EXPERTS])
        g1_ = sb("g1", [128, HALVES, TILES])
        g2_ = sb("g2", [128, HALVES, TILES])
        mr_ = sb("mr", [128, HALVES, TILES])
        ex_ = sb("ex", [128, HALVES, TILES])
        gpart = sb("gpart", [128, NT, 128], f16)
        gateT = sb("gateT", [128, TOKENS], f16)
        NB = 4
        high_parts = sb("high_parts", [128, 6 * 512], f32r)
        low_parts = sb("low_parts", [128, 6 * 512], f32r)
        hidden = sb("hidden", [128, 2 * NB * 512])

        def buffers(t, first, n):
            return [t[:, k * 512:(k + 1) * 512] for k in range(first, first + n)]

        h_hi, w_hi = buffers(high_parts, 0, NB), buffers(high_parts, NB, 2)
        h_lo, w_lo = buffers(low_parts, 0, NB), buffers(low_parts, NB, 2)
        ge, hm = buffers(hidden, 0, NB), buffers(hidden, NB, NB)
        yT = xT
        x3 = sb("x3", [128, 8, D])
        qe, qn, qmax, inv, qeT, ao, aoT = [], [], [], [], [], [], []
        for h in range(HALVES):
            qe.append(sb(f"qe{h}", [128, 512]))
            qn.append(sb(f"qn{h}", [128, 512]))
            qmax.append(sb(f"qmax{h}", [128, TILES * HEADS]))
            inv.append(sb(f"inv{h}", [128, TILES, 2, HEADS]))
            qeT.append(hidden[:, h * 512:(h + 1) * 512])
            ao.append(hidden[:, (2 + h) * 512:(3 + h) * 512])
            aoT.append(hidden[:, (4 + h) * 512:(5 + h) * 512])
        x4 = sb("x4", [128, 8, D])
        x4T = sb("x4T", [128, TOKENS])
        wb_max = sb("wb_max", [128, 3 * IC * NBLK])
        wb_s = sb("wb_s", [128, 3 * IC * NBLK])
        wb_r = sb("wb_r", [128, 3 * IC * NBLK])
        wb_i = sb("wb_i", [128, 3 * IC, D])
        wb_d = wb_i
        wT = sb("wT", [128, 3 * IC, D])
        wT_hi = sb("wT_hi", [128, 3 * IC, D], f32r)
        wT_lo = sb("wT_lo", [128, 3 * IC, D], f32r)
        nx = sb("nx", [128, TOKENS], i16)
        gq = sb("gq", [128, IC, TOKENS])
        up = sb("up", [128, IC, TOKENS])
        ng = sb("ng", [128, IC, TOKENS], i16)
        def third(t, dt=None):
            t = t if dt is None else t.bitcast(dt)
            return t.rearrange("p (c n) -> p c n", c=IC)

        nu = third(wexp[:, 0:1536], i16)
        sq = third(wexp[:, 1536:3072], u16)
        sg = third(hidden[:, 0:3072])
        pg = sg
        n3 = ng
        og = gq
        n4 = nu
        o_hi = third(high_parts[:, :])
        o_lo = third(low_parts[:, :])
        res = hidden[:, 3072:4096]
        STG = ("x", "g", "u", "p", "o")
        amax = {k: sb(f"amax_{k}", [128, 6]) for k in STG}
        amax1 = {k: sb(f"amax1_{k}", [128, 1]) for k in STG}
        gmax = {k: sb(f"gmax_{k}", [128, 1]) for k in STG}
        scale = {k: sb(f"scale_{k}", [128, 1]) for k in STG}
        rcp = {k: sb(f"rcp_{k}", [128, 1]) for k in STG}
        mul = {k: sb(f"mul_{k}", [128, 1]) for k in STG}
        unit = {k: sb(f"unit_{k}", [128, 1]) for k in STG}
        unitq = {k: sb(f"unitq_{k}", [128, 1]) for k in STG}
        tscale = sb("tscale", [128, 1])
        warm = sb("warm", [1, 2])

        x_in = [sem(f"x_in{h}") for h in range(HALVES)]
        pa_in, pb_in, row_in, exp_in, lpbq_in, out_done = map(
            sem, ("pa_in", "pb_in", "row_in", "exp_in", "lpbq_in", "out_done"))
        const_ready, const_late, pool_step = map(sem, ("const_ready", "const_late", "pool_step"))
        dve_step, zero_ready = map(sem, ("dve_step", "zero_ready"))
        kT_mm, kT_ready, v0_mm, v0_ready, g_mm, tg_ready = map(
            sem, ("kT_mm", "kT_ready", "v0_mm", "v0_ready", "g_mm", "tg_ready"))
        wqk_mm, wqk_ready, kv1_mm, k1_ready, v1_ready, k1_soft = map(
            sem, ("wqk_mm", "wqk_ready", "kv1_mm", "k1_ready", "v1_ready", "k1_soft"))
        kv_mm, kv_raw_ready, kv_ready = map(sem, ("kv_mm", "kv_raw_ready", "kv_ready"))
        var_ready, rstd_ready, xn_ready, xT_mm, xT_ready = map(
            sem, ("var_ready", "rstd_ready", "xn_ready", "xT_mm", "xT_ready"))
        s_mm, s_sub, shift_ready, xn_act, pr_ready, prT_mm, prT_ready, pv_mm, x2_ready = map(
            sem, ("s_mm", "s_sub", "shift_ready", "xn_act", "pr_ready", "prT_mm", "prT_ready", "pv_mm", "x2_ready"))
        xhi_ready, xlo_ready, rw_ready, lg_mm, lg_read, dm_ready, ex_ready = map(
            sem, ("xhi_ready", "xlo_ready", "rw_ready", "lg_mm", "lg_read", "dm_ready", "ex_ready"))
        gpart_ready, gateT_mm, gateT_ready = map(sem, ("gpart_ready", "gateT_mm", "gateT_ready"))
        w1_split, w2_split, z_ready, gb_ready = map(
            sem, ("w1_split", "w2_split", "z_ready", "gb_ready"))
        gelu_done, gated, hi_done, lo_done, y_done = map(
            sem, ("gelu_done", "gated", "hi_done", "lo_done", "y_done"))
        yT_ready, yN_mm, x3_ready = map(sem, ("yT_ready", "yN_mm", "x3_ready"))
        q_mm, q_sub, qe_ready, qeT_mm, qeT_ready, inv_ready, qn_ready = map(
            sem, ("q_mm", "q_sub", "qe_ready", "qeT_mm", "qeT_ready", "inv_ready", "qn_ready"))
        nd_mm, ao_ready, aoT_mm, aoT_ready, proj_mm, x4_ready = map(
            sem, ("nd_mm", "ao_ready", "aoT_mm", "aoT_ready", "proj_mm", "x4_ready"))
        x4T_mm, x4T_ready, wb_scale, wb_ready, wT_mm, wT_ready, wT_split = map(
            sem, ("x4T_mm", "x4T_ready", "wb_scale", "wb_ready", "wT_mm", "wT_ready", "wT_split"))
        amax_ready = {k: sem(f"amax_ready_{k}") for k in STG}
        gmax_ready = {k: sem(f"gmax_ready_{k}") for k in STG}
        mul_ready = {k: sem(f"mul_ready_{k}") for k in STG}
        pg_ready, og_ready, n3_ready = map(sem, ("pg_ready", "og_ready", "n3_ready"))
        nx_ready, xq_ready, gu_mm, gu_ready, gu_free = map(sem, ("nx_ready", "xq_ready", "gu_mm", "gu_ready", "gu_free"))
        ng_ready, sg_ready, sq_ready, nu_ready, n4_ready, ohi_ready, olo_ready = map(
            sem, ("ng_ready", "sg_ready", "sq_ready", "nu_ready", "n4_ready", "ohi_ready", "olo_ready"))
        dn_mm, res_ready = map(sem, ("dn_mm", "res_ready"))

        CREDIT = 8

        def half(t, h):
            return t[:, h * HT:(h + 1) * HT]

        def tiles(t, h):
            return t[:, h * TILES:(h + 1) * TILES, :]

        def by_head(t):
            return t[:, :].rearrange("p (a c) -> p a c", c=HD)

        block = ctx.enter_context(nc.Block())

        @block.sync
        def _(sp):
            xv = x.rearrange("b (t p) d -> p (b t) d", p=128)
            sp.dma_start(xin[:, 0:TILES, :], xv[:, 0:TILES, :]).then_inc(x_in[0], 16)
            sp.dma_start(pa[:, :], packa).then_inc(pa_in, 16)
            sp.dma_start(xin[:, TILES:, :], xv[:, TILES:, :]).then_inc(x_in[1], 16)
            sp.dma_start(pb[:, :], packb).then_inc(pb_in, 16)
            sp.dma_start(wq4[:, :, :], lpbq).then_inc(lpbq_in, 16)
            sp.dma_start(wexp[:, :], experts).then_inc(exp_in, 16)
            for h in range(HALVES):
                sp.wait_ge(res_ready, h + 1)
                sp.dma_start(half(out, h), half(res, h)).then_inc(out_done, 16)
            sp.wait_ge(out_done, 16 * HALVES)

        @block.gpsimd
        def _(pool):
            steps = [0]

            def step(ins):
                steps[0] += 1
                ins.then_inc(pool_step, 1)
                return steps[0]

            def link(ins):
                pool.wait_ge(pool_step, step(ins))

            def rstd_of(n):
                pool.wait_ge(var_ready, n)
                h = (n - 1) % HALVES
                pool.tensor_tensor(rstd[:, h, :], var[:, h, :], neg_half[:, :], ALU.pow).then_inc(rstd_ready, 1)

            pool.memset(ident[:, :], 0.0)
            pool.memset(ones[:, :], 1.0)
            link(pool.memset(neg_half[:, :], -0.5))
            link(pool.affine_select(out=ident[:, :], in_=ident[:, :], compare_op=ALU.not_equal, fill=1.0,
                                    base=0, pattern=[[-1, 128]], channel_multiplier=1))
            pool.drain().then_inc(const_ready, 1)
            pool.memset(gpart[:, :, :], 0.0)
            pool.memset(v1[:, :, D:D + 1], 1.0)
            pool.tensor_tensor(ident16[:, :], ident[:, :], ident[:, :], ALU.mult)
            pool.iota(number[:, :], pattern=[[1, EXPERTS]], base=0, channel_multiplier=0,
                      allow_small_or_imprecise_dtypes=True)
            rstd_of(1)
            rstd_of(2)
            link(pool.memset(sel[:, :, :], 0.0))
            for part in range(2):
                link(pool.affine_select(out=sel[:, :, :], in_=sel[:, :, :], compare_op=ALU.not_equal,
                                        fill=1.0, base=-EXPERTS * part,
                                        pattern=[[-1, EXPERTS], [0, 128]], channel_multiplier=1))
            link(pool.memset(head_mask[:, :, :], 1.0))
            link(pool.affine_select(out=head_mask[:, :, :], in_=head_mask[:, :, :], compare_op=ALU.is_ge,
                                    fill=0.0, base=0, pattern=[[-HD, HEADS], [0, HD]],
                                    channel_multiplier=1))
            link(pool.affine_select(out=head_mask[:, :, :], in_=head_mask[:, :, :], compare_op=ALU.is_ge,
                                    fill=0.0, base=HD - 1, pattern=[[HD, HEADS], [0, HD]],
                                    channel_multiplier=-1))
            for b in range(BATCH):
                pool.tensor_tensor(kc[:, b, 1, :], head_mask[:, :, 0], head_mask[:, :, 0], ALU.mult)
            pool.wait_ge(row_in, 16)
            pool.tensor_tensor(ones_r[:, :], ones[0:1, 0:128], ones[0:1, 0:128], ALU.mult)
            for k, name in enumerate(("bq1", "bp1")):
                link(pool.tensor_tensor(row_hi[:, k, :], R(name), ones[0:1, 0:128], ALU.mult))
                pool.tensor_tensor(row_lo[:, k, :], R(name), row_hi[:, k, :].bitcast(f32), ALU.subtract)
            pool.drain().then_inc(const_late, 1)
            rstd_of(3)
            rstd_of(4)

            def split_pair(i):
                for odd in range(2):
                    e = 2 * i + odd
                    for w2, (free, done) in enumerate(((z_ready, w1_split), (y_done, w2_split))):
                        pool.wait_ge(free, CREDIT + 4 * e - 4)
                        cols = 256 * w2
                        raw = wexp[:, bass.ds(e * 512 + cols, 256)]
                        hi, lo = w_hi[odd][:, cols:cols + 256], w_lo[odd][:, cols:cols + 256]
                        pool.tensor_tensor(hi, raw, ones[:, 0:256], ALU.mult)
                        pool.drain()
                        pool.tensor_tensor(lo, raw, hi.bitcast(f32), ALU.subtract).then_inc(done, 1)

            pool.wait_ge(exp_in, 16)
            split_pair(0)

            pool.wait_ge(wb_scale, 1)
            blocks = wq4[:, :, :].rearrange("p c (b k) -> p (c b) k", k=QBLOCK)
            shape = [128, 3 * IC * NBLK, QBLOCK]
            ints = wb_i[:, :, :].rearrange("p c (b k) -> p (c b) k", k=QBLOCK)
            link(pool.tensor_tensor(ints, blocks, wb_r[:, :].unsqueeze(2).broadcast_to(shape), ALU.mult))
            link(pool.tensor_scalar(wb_i[:, :, :], wb_i[:, :, :], ROUND, -ROUND, ALU.add, ALU.add))
            pool.tensor_tensor(ints, ints, wb_s[:, :].unsqueeze(2).broadcast_to(shape), ALU.mult)\
                .then_inc(wb_ready, 1)
            with pool.Fori(1, EXPERTS // 2) as i:
                split_pair(i)
            rstd_of(5)
            rstd_of(6)
            mask = head_mask[:, :, 0]
            for k in range(BPH):
                pool.wait_ge(kv_raw_ready, k + 1)
                for h in range(HALVES):
                    b = h * BPH + k
                    pool.tensor_tensor(kv[:, b, :], kv_raw[:, k, h, 0:D],
                                       head_mask[:, :, :].rearrange("p a b -> p (a b)"), ALU.mult)
                    pool.tensor_tensor(kc[:, b, 0, :], kv_raw[:, k, h, D:D + 1].broadcast_to([128, HEADS]), mask,
                                       ALU.mult)
            pool.drain().then_inc(kv_ready, 1)
            for c in range(IC):
                pool.wait_ge(wT_ready, c + 1)
                k = slice(IC * c, IC * c + IC)
                pool.tensor_tensor(wT_lo[:, k, :], wT[:, k, :], wT_hi[:, k, :].bitcast(f32), ALU.subtract)\
                    .then_inc(wT_split, 1)
            for h in range(HALVES):
                pool.wait_ge(inv_ready, h + 1)
                r = inv[h][:, :, 1, :]
                for t in range(TILES):
                    last = pool.tensor_tensor(by_head(qn[h])[:, t * HEADS:(t + 1) * HEADS, :],
                                              by_head(qe[h])[:, t * HEADS:(t + 1) * HEADS, :],
                                              r[:, t, :].unsqueeze(2).broadcast_to([128, HEADS, HD]), ALU.mult)
                last.then_inc(qn_ready, 1)
            rstd_of(7)
            rstd_of(8)
            for k in STG:
                pool.wait_ge(amax_ready[k], 1)
                pool.partition_all_reduce(gmax[k][:, :], amax1[k][:, :], 128, bass.bass_isa.ReduceOp.absmax)\
                    .then_inc(gmax_ready[k], 1)

        @block.scalar
        def _(act):
            act.sem_inc(gelu_done, CREDIT)
            act.sem_inc(hi_done, CREDIT)

            def evac(dst, src, ready, n, done):
                act.wait_ge(ready, n)
                act.activation(dst, src, ACT.Copy).then_inc(done, 1)

            def normalise(src, n):
                h = (n - 1) % HALVES
                if n > 2:
                    act.wait_ge(xT_mm, n - 2)
                act.wait_ge(shift_ready, n)
                for t in range(TILES // 2, TILES):
                    last = act.activation(xn[:, h * TILES + t, :], src[:, h * TILES + t, :], ACT.Identity,
                                          bias=shift[:, h, t:t + 1], scale=rstd[:, h, t:t + 1])
                last.then_inc(xn_act, 1)

            act.dma_start(row[:, :], rows).then_inc(row_in, 16)
            act.wait_ge(g_mm, 1)
            act.activation(tg[:, :], bank[2][:, 0:4], ACT.Tanh).then_inc(tg_ready, 1)
            act.wait_ge(kT_mm, 1)
            act.activation(kT[:, :], bank[0][:, 0:256], ACT.Identity, bias=A("bk", 1)).then_inc(kT_ready, 1)
            normalise(xin, 1)
            act.wait_ge(wqk_mm, 1)
            act.activation(wqk[:, :], bank[1][:, 0:256], ACT.Copy)
            act.activation(bqk[:, :], bank[0][0:1, 0:256], ACT.Copy).then_inc(wqk_ready, 1)
            evac(half(xT, 0), bank[6][:, :], xT_mm, 1, xT_ready)
            normalise(xin, 2)
            evac(half(xT, 1), bank[7][:, :], xT_mm, 2, xT_ready)
            for h in range(HALVES):
                act.wait_ge(s_sub, h + 1)
                act.activation(sc[:, h, :, :], sc[:, h, :, :], ACT.Exp).then_inc(pr_ready, 1)
                if h == 0:
                    evac(v0[:, :, :].rearrange("p b d -> p (b d)"), bank[3][:, 0:256], v0_mm, 1, v0_ready)
                evac(prT[:, h, :, :].rearrange("p t d -> p (t d)"), bank[2 + h][:, 0:256],
                     prT_mm, h + 1, prT_ready)
            act.wait_ge(kv1_mm, 1)
            act.activation(k1[:, :, :].rearrange("p b d -> p (b d)"), bank[2][:, 0:256], ACT.Copy)
            act.activation(v1[:, :, 0:D], bank[2][:, 256:512].rearrange("p (h d) -> p h d", d=D), ACT.Copy)\
                .then_inc(k1_ready, 1)
            for h in range(HALVES):
                normalise(x2, 3 + h)
                evac(half(xhi, h), bank[h][:, :], xT_mm, 3 + h, xhi_ready)
            act.wait_ge(k1_soft, 1)
            act.activation(k1e[:, :, :], k1[:, :, :], ACT.Exp).then_inc(k1_soft, 1)

            def gate_columns(h):
                evac(half(gateT, h), bank[2 + h][:, 0:256].bitcast(f16), gateT_mm, h + 1, gateT_ready)

            for h in range(HALVES):
                act.wait_ge(dm_ready, h + 1)
                act.activation(ex_[:, h, :], g2_[:, h, :], ACT.Exp).then_inc(ex_ready, 1)
                if h == 0:
                    gate_columns(0)
            act.activation(warm[:, 0:1], row[0:1, 0:1], ACT.Gelu)

            def gelu(u, j):
                act.wait_ge(z_ready, CREDIT + u + 1)
                act.wait_ge(gated, CREDIT + u - NB + 1)
                act.activation(ge[j % NB][:, :], bank[4 + j % NB][:, :], ACT.Gelu).then_inc(gelu_done, 1)

            def high(u, j):
                act.wait_ge(gated, CREDIT + u + 1)
                act.wait_ge(y_done, CREDIT + u - NB + 1)
                act.activation(h_hi[j % NB][:, :], hm[j % NB][:, :], ACT.Copy).then_inc(hi_done, 1)

            def units(i, last):
                for j in range(8):
                    if not (last and j == 7):
                        gelu(8 * i + j + 1, j + 1)
                    high(8 * i + j, j)

            gelu(0, 0)
            gate_columns(1)
            with act.Fori(0, EXPERTS // 2 - 1) as i:
                units(i, False)
            units(EXPERTS // 2 - 1, True)

            for h in range(HALVES):
                evac(half(yT, h), bank[h][:, :], y_done, CREDIT + 30 + 2 * h, yT_ready)
            act.activation(warm[:, 1:2], row[0:1, 0:1], ACT.Exp)
            for c in range(IC):
                act.wait_ge(wT_mm, c + 1)
                src = bank[2 + c % 2][:, 0:IC * D].rearrange("p (c d) -> p c d", d=D)
                k = slice(IC * c, IC * c + IC)
                act.activation(wT_hi[:, k, :], src, ACT.Copy)
                act.activation(wT[:, k, :], src, ACT.Copy).then_inc(wT_ready, 1)
            for h in range(HALVES):
                normalise(x3, 5 + h)
                evac(half(xT, h), bank[6 + h][:, :], xT_mm, 5 + h, xT_ready)
                if h == 0:
                    for k in range(BPH):
                        act.wait_ge(kv_mm, k + 1)
                        act.activation(kv_raw[:, k, :, :].rearrange("p h d -> p (h d)"),
                                       bank[2 + k][:, 0:HALVES * (D + 1)], ACT.Copy).then_inc(kv_raw_ready, 1)
            for h in range(HALVES):
                act.wait_ge(q_sub, h + 1)
                act.activation(qe[h][:, :], qe[h][:, :], ACT.Exp).then_inc(qe_ready, 1)
                evac(qeT[h], bank[4 + h][:, :], qeT_mm, h + 1, qeT_ready)
            for h in range(HALVES):
                evac(aoT[h], bank[4 + h][:, :], aoT_mm, h + 1, aoT_ready)
            act.activation(warm[:, 0:1], row[0:1, 0:1], ACT.Sigmoid)
            for h in range(HALVES):
                normalise(x4, 7 + h)
            for h in range(HALVES):
                evac(half(x4T, h), bank[4 + h][:, :], x4T_mm, h + 1, x4T_ready)
            act.wait_ge(mul_ready["x"], 1)
            for h in range(HALVES):
                act.wait_ge(xT_mm, 7 + h)
                act.activation(half(nx, h), bank[6 + h][:, :], ACT.Copy, scale=mul["x"][:, :]).then_inc(xq_ready, 1)

            def product(n):
                c, h = n // HALVES, n % HALVES
                dst = gq if c < IC else up
                act.wait_ge(gu_mm, n + 1)
                act.activation(half(dst[:, c % IC, :], h), bank[n % 6][:, :], ACT.Copy).then_inc(gu_ready, 1)

            for n in range(IC * HALVES + 2):
                product(n)
            act.wait_ge(mul_ready["g"], 1)
            for c in range(IC):
                act.activation(ng[:, c, :], gq[:, c, :], ACT.Copy, scale=mul["g"][:, :]).then_inc(ng_ready, 1)
                act.wait_ge(ng_ready, c + 1)
                act.activation(sg[:, c, :], ng[:, c, :], ACT.Sigmoid, scale=scale["g"][:, :])\
                    .then_inc(sg_ready, 1)
                for k in range(2 if c < 2 else 0):
                    product(IC * HALVES + 2 + 2 * c + k)
            act.wait_ge(mul_ready["u"], 1)
            for c in range(IC):
                act.activation(nu[:, c, :], up[:, c, :], ACT.Copy, scale=mul["u"][:, :]).then_inc(nu_ready, 1)
            act.wait_ge(mul_ready["p"], 1)
            for c in range(1, IC):
                act.activation(n3[:, c, :], pg[:, c, :], ACT.Copy, scale=mul["p"][:, :]).then_inc(n3_ready, 1)
            act.wait_ge(mul_ready["o"], 1)
            for n in range(IC * HALVES):
                c, h = n // HALVES, n % HALVES
                act.activation(half(n4[:, c, :], h), half(og[:, c, :], h), ACT.Copy, scale=mul["o"][:, :])\
                    .then_inc(n4_ready, 1)
                if h == 1:
                    act.wait_ge(n4_ready, n + 1)
                    act.activation(half(o_hi[:, c, :], h), half(n4[:, c, :], h), ACT.Copy).then_inc(ohi_ready, 1)

        @block.vector
        def _(dve):
            steps = [0]

            def step(ins):
                steps[0] += 1
                ins.then_inc(dve_step, 1)
                return steps[0]

            def link(ins):
                dve.wait_ge(dve_step, step(ins))

            dve.memset(zero16[:, :], 0.0).then_inc(zero_ready, 1)
            dve.sem_inc(gated, CREDIT)
            dve.sem_inc(lo_done, CREDIT)

            def statistics(src, h):
                for t in range(TILES):
                    m = step(dve.bn_stats(stats[:, h, t, :], src[:, h * TILES + t, :]))
                dve.wait_ge(dve_step, m)
                for t in range(TILES):
                    m = step(dve.bn_aggr(mv[:, h, t, :], stats[:, h, t, :]))
                dve.wait_ge(dve_step, m)
                dve.tensor_scalar(var[:, h, :], mv[:, h, :, 1], LN_EPS, None, ALU.add).then_inc(var_ready, 1)

            def normalise(src, n):
                h = (n - 1) % HALVES
                dve.wait_ge(rstd_ready, n)
                dve.scalar_tensor_tensor(out=shift[:, h, :], in0=mv[:, h, :, 0], scalar=-1.0,
                                         in1=rstd[:, h, :], op0=ALU.mult, op1=ALU.mult).then_inc(shift_ready, 1)
                if n > 2:
                    dve.wait_ge(xT_mm, n - 2)
                for t in range(TILES // 2):
                    last = dve.tensor_scalar(xn[:, h * TILES + t, :], src[:, h * TILES + t, :],
                                             mv[:, h, t, 0:1], rstd[:, h, t:t + 1], ALU.subtract, ALU.mult)
                last.then_inc(xn_ready, 1)

            def weight_scales():
                dve.wait_ge(lpbq_in, 16)
                link(dve.tensor_reduce(wb_max[:, :], wq4[:, :, :].rearrange("p c (b k) -> p (c b) k", k=QBLOCK),
                                       X, ALU.max, apply_absolute_value=True))
                link(dve.tensor_scalar(wb_s[:, :], wb_max[:, :], 1.0 / WQMAX, QMIN_SCALE, ALU.mult, ALU.max))
                dve.reciprocal(wb_r[:, :], wb_s[:, :]).then_inc(wb_scale, 1)

            def scores(h):
                s = bank[h][:, 0:TILES * CTX].rearrange("p (t c) -> p t c", c=CTX)
                dve.wait_ge(s_mm, h + 1)
                link(dve.tensor_reduce(smax[:, h, :], s, X, ALU.max))
                dve.tensor_tensor(sc[:, h, :, :], s, smax[:, h, :].unsqueeze(2).broadcast_to([128, TILES, CTX]),
                                  ALU.subtract).then_inc(s_sub, 1)

            def add_attention(h):
                dve.wait_ge(pr_ready, h + 1)
                link(dve.tensor_reduce(ssum[:, h, :], sc[:, h, :, :], X, ALU.add))
                link(dve.reciprocal(smax[:, h, :], ssum[:, h, :]))
                link(dve.tensor_scalar(ssum[:, h, :], smax[:, h, :], tg[:, G_XATTN0:G_XATTN0 + 1], None, ALU.mult))
                dve.wait_ge(pv_mm, h + 1)
                for t in range(TILES):
                    b, k = t // TPB, t % TPB
                    slot = k * BPH + b
                    last = dve.scalar_tensor_tensor(out=x2[:, h * TILES + t, :],
                                                    in0=bank[4 + 2 * h + b][:, k * D:(k + 1) * D],
                                                    scalar=ssum[:, h, slot:slot + 1],
                                                    in1=xin[:, h * TILES + t, :], op0=ALU.mult, op1=ALU.add)
                link(last)

            def low_tokens(h):
                dve.wait_ge(xhi_ready, h + 1)
                dve.tensor_tensor(half(xlo, h), bank[h][:, :], half(xhi, h).bitcast(f32), ALU.subtract)\
                    .then_inc(xlo_ready, 1)

            def route(h):
                wide = [128, TILES, EXPERTS]
                lg, best, place, top1, top2, gate = (tiles(t, h) for t in (lg_, best_, place_, top1_, top2_, gate_))
                mr, g1, g2, ex = (t[:, h, :] for t in (mr_, g1_, g2_, ex_))

                def over(t):
                    return t.broadcast_to(wide)

                order = number[:, :].unsqueeze(1).broadcast_to(wide)
                dve.wait_ge(const_late, 1)
                dve.wait_ge(lg_mm, h + 1)
                dve.tensor_copy(lg, bank[2 + h][:, 0:TILES * EXPERTS].rearrange("p (t e) -> p t e", e=EXPERTS))\
                    .then_inc(lg_read, 1)
                dve.wait_ge(lg_read, h + 1)
                for t in range(TILES):
                    n = step(dve.max(best[:, t, :], lg[:, t, :]))
                dve.wait_ge(dve_step, n)
                dve.tensor_tensor(g2, best[:, :, 1], best[:, :, 0], ALU.subtract).then_inc(dm_ready, 1)
                for t in range(TILES):
                    n = step(dve.max_index(place[:, t, :], best[:, t, :], lg[:, t, :]))
                dve.wait_ge(dve_step, n)
                dve.tensor_tensor(top1, order, over(place[:, :, 0:1]), ALU.is_equal)
                dve.tensor_tensor(top2, order, over(place[:, :, 1:2]), ALU.is_equal)
                dve.wait_ge(ex_ready, h + 1)
                link(dve.tensor_scalar(mr, ex, 1.0, None, ALU.add))
                link(dve.reciprocal(g1, mr))
                dve.tensor_tensor(top1, top1, over(g1.unsqueeze(2)), ALU.mult)
                link(dve.tensor_tensor(g2, g1, ex, ALU.mult))
                link(dve.tensor_tensor(top2, top2, over(g2.unsqueeze(2)), ALU.mult))
                link(dve.tensor_tensor(gate, top1, top2, ALU.add))
                high, low = (tiles(gpart, h)[:, :, EXPERTS * k:EXPERTS * (k + 1)] for k in range(2))
                link(dve.tensor_copy(high, gate))
                dve.tensor_tensor(low, gate, high, ALU.subtract).then_inc(gpart_ready, 1)

            def keys_by_head(t):
                return t[:, :, :].rearrange("p b (a c) -> p (b a) c", c=HD)

            kwide = [128, HALVES * HEADS, HD]

            def keys_less_max():
                dve.wait_ge(k1_ready, 1)
                link(dve.tensor_reduce(k1max[:, :], keys_by_head(k1), X, ALU.max))
                dve.tensor_tensor(keys_by_head(k1), keys_by_head(k1),
                                  k1max[:, :].unsqueeze(2).broadcast_to(kwide), ALU.subtract).then_inc(k1_soft, 1)

            def keys_softmax():
                dve.wait_ge(k1_soft, 2)
                link(dve.tensor_reduce(k1sum[:, :], keys_by_head(k1e), X, ALU.add))
                link(dve.reciprocal(k1max[:, :], k1sum[:, :]))
                dve.tensor_tensor(keys_by_head(k1), keys_by_head(k1e),
                                  k1max[:, :].unsqueeze(2).broadcast_to(kwide), ALU.mult).then_inc(k1_soft, 1)

            for h in range(HALVES):
                dve.wait_ge(x_in[h], 16)
                statistics(xin, h)
            normalise(xin, 1)
            normalise(xin, 2)
            dve.wait_ge(pa_in, 16)
            link(dve.tensor_copy(rw_hi[:, :], A("rwT", EXPERTS)))
            dve.tensor_tensor(rw_lo[:, :], A("rwT", EXPERTS), rw_hi[:, :].bitcast(f32), ALU.subtract)\
                .then_inc(rw_ready, 1)
            weight_scales()
            dve.wait_ge(tg_ready, 1)
            scores(0)
            scores(1)
            add_attention(0)
            statistics(x2, 0)
            add_attention(1)
            normalise(x2, 3)
            statistics(x2, 1)
            low_tokens(0)
            normalise(x2, 4)
            keys_less_max()
            low_tokens(1)
            route(0)
            keys_softmax()
            route(1)

            def gate_unit(i, j):
                u = 8 * i + j
                dve.wait_ge(gelu_done, CREDIT + u + 1)
                if j % FC == 0:
                    dve.wait_ge(gb_ready, 4 * i + j // FC + 1)
                dve.wait_ge(hi_done, CREDIT + u - NB + 1)
                dve.tensor_tensor(hm[j % NB][:, :], ge[j % NB][:, :], bank[2 + (j // FC) % 2][:, :], ALU.mult)\
                    .then_inc(gated, 1)

            def low(u, j):
                dve.wait_ge(hi_done, CREDIT + u + 1)
                dve.wait_ge(y_done, CREDIT + u - NB + 1)
                dve.tensor_tensor(h_lo[j % NB][:, :], hm[j % NB][:, :], h_hi[j % NB][:, :].bitcast(f32),
                                  ALU.subtract).then_inc(lo_done, 1)

            def units(i, last):
                for j in range(8):
                    if not (last and j == 7):
                        gate_unit(i, j + 1)
                    low(8 * i + j, j)

            gate_unit(0, 0)
            with dve.Fori(0, EXPERTS // 2 - 1) as i:
                units(i, False)
            units(EXPERTS // 2 - 1, True)

            def add_experts(h):
                dve.wait_ge(yN_mm, h + 1)
                dve.scalar_tensor_tensor(out=tiles(x3, h).rearrange("p t d -> p (t d)"), in0=bank[4 + h][:, :],
                                         scalar=tg[:, G_FFN0:G_FFN0 + 1],
                                         in1=tiles(x2, h).rearrange("p t d -> p (t d)"),
                                         op0=ALU.mult, op1=ALU.add).then_inc(x3_ready, 1)
                dve.wait_ge(x3_ready, h + 1)

            wide = [128, TILES * HEADS, HD]

            def q_less_max(h):
                dve.wait_ge(q_mm, h + 1)
                link(dve.tensor_reduce(qmax[h][:, :], by_head(bank[h]), X, ALU.max))
                dve.tensor_tensor(by_head(qe[h]), by_head(bank[h]), qmax[h][:, :].unsqueeze(2).broadcast_to(wide),
                                  ALU.subtract).then_inc(q_sub, 1)

            def attention(h):
                dve.wait_ge(nd_mm, h + 1)
                dve.reciprocal(inv[h][:, :, :, :].rearrange("p t k a -> p (t k a)"),
                               bank[h][:, 0:TILES * 2 * HEADS]).then_inc(inv_ready, 1)
                dve.wait_ge(inv_ready, h + 1)
                for t in range(TILES):
                    n = step(dve.tensor_tensor(by_head(ao[h])[:, t * HEADS:(t + 1) * HEADS, :],
                                               by_head(bank[6 + h])[:, t * HEADS:(t + 1) * HEADS, :],
                                               inv[h][:, t, 0, :].unsqueeze(2).broadcast_to([128, HEADS, HD]),
                                               ALU.mult))
                dve.wait_ge(dve_step, n)
                dve.wait_ge(qn_ready, h + 1)
                dve.tensor_tensor(ao[h], ao[h], qn[h][:, :], ALU.add).then_inc(ao_ready, 1)

            def add_linear_attention(h):
                dve.wait_ge(proj_mm, h + 1)
                dve.scalar_tensor_tensor(out=tiles(x4, h).rearrange("p t d -> p (t d)"), in0=bank[2 + h][:, :],
                                         scalar=tg[:, G_XATTN1:G_XATTN1 + 1],
                                         in1=tiles(x3, h).rearrange("p t d -> p (t d)"),
                                         op0=ALU.mult, op1=ALU.add).then_inc(x4_ready, 1)
                dve.wait_ge(x4_ready, h + 1)

            add_experts(0)
            statistics(x3, 0)
            add_experts(1)
            normalise(x3, 5)
            statistics(x3, 1)
            normalise(x3, 6)
            for h in range(HALVES):
                q_less_max(h)
            for h in range(HALVES):
                attention(h)
            add_linear_attention(0)
            statistics(x4, 0)
            add_linear_attention(1)
            normalise(x4, 7)
            statistics(x4, 1)
            normalise(x4, 8)
            for h in range(HALVES):
                dve.wait_ge(xn_ready, 7 + h)
                dve.wait_ge(xn_act, 7 + h)
                step(dve.tensor_reduce(amax["x"][:, h:h + 1], tiles(xn, h).rearrange("p t d -> p (t d)"),
                                       X, ALU.max, apply_absolute_value=True))

            def max_over(k, n):
                dve.wait_ge(dve_step, steps[0])
                dve.tensor_reduce(amax1[k][:, :], amax[k][:, 0:n], X, ALU.max).then_inc(amax_ready[k], 1)

            def make_scale(k):
                dve.wait_ge(gmax_ready[k], 1)
                if k == "x":
                    link(dve.tensor_scalar(scale[k][:, :], gmax[k][:, :], 1.0 / QMAX, QMIN_SCALE,
                                           ALU.mult, ALU.max))
                    dve.reciprocal(mul[k][:, :], scale[k][:, :]).then_inc(mul_ready[k], 1)
                    return
                link(dve.tensor_scalar(scale[k][:, :], gmax[k][:, :], unitq[k][:, :], QMIN_SCALE,
                                       ALU.mult, ALU.max))
                link(dve.reciprocal(rcp[k][:, :], scale[k][:, :]))
                dve.tensor_tensor(mul[k][:, :], rcp[k][:, :], unit[k][:, :], ALU.mult).then_inc(mul_ready[k], 1)

            def make_unit(k, a, b):
                link(dve.tensor_scalar(unit[k][:, :], a, b, None, ALU.mult))
                link(dve.tensor_scalar(unitq[k][:, :], unit[k][:, :], 1.0 / QMAX, None, ALU.mult))

            def product_max(k, n):
                base, t = (0, gq) if k == "g" else (IC * HALVES, up)
                dve.wait_ge(gu_ready, base + n + 1)
                step(dve.tensor_reduce(amax[k][:, n:n + 1], half(t[:, n // HALVES, :], n % HALVES),
                                       X, ALU.max, apply_absolute_value=True))

            max_over("x", HALVES)
            make_scale("x")
            dve.wait_ge(mul_ready["x"], 1)
            for h in range(HALVES):
                dve.wait_ge(xq_ready, h + 1)
                link(dve.tensor_copy(half(xhi, h), half(nx, h)))
                dve.tensor_tensor(half(xlo, h), half(nx, h), half(xhi, h).bitcast(f32), ALU.subtract)\
                    .then_inc(nx_ready, 1)
            for k in ("g", "u"):
                make_unit(k, scale["x"][:, :], 1.0)
            for n in range(IC * HALVES):
                product_max("g", n)
            max_over("g", IC * HALVES)
            make_scale("g")
            dve.wait_ge(mul_ready["g"], 1)
            make_unit("p", scale["g"][:, :], 1.0 / SIG_STEPS)
            product_max("u", 0)
            product_max("u", 1)
            for c in range(IC):
                dve.wait_ge(sg_ready, c + 1)
                link(dve.tensor_scalar(sq[:, c, :], sg[:, c, :], SIG_STEPS, None, ALU.mult))
                m = step(dve.tensor_tensor(pg[:, c, :], ng[:, c, :], sq[:, c, :], ALU.mult))
                dve.wait_ge(dve_step, m)
                step(dve.tensor_reduce(amax["p"][:, c:c + 1], pg[:, c, :], X, ALU.max,
                                       apply_absolute_value=True))
                if c < 2:
                    product_max("u", 2 + 2 * c)
                    product_max("u", 3 + 2 * c)
                if c == 1:
                    max_over("u", IC * HALVES)
            max_over("p", IC)
            make_scale("u")
            make_scale("p")
            dve.wait_ge(mul_ready["p"], 1)
            make_unit("o", scale["p"][:, :], scale["u"][:, :])
            for c in range(IC):
                if c == 0:
                    link(dve.tensor_scalar(n3[:, c, :], pg[:, c, :], mul["p"][:, :], None, ALU.mult))
                else:
                    dve.wait_ge(n3_ready, c)
                dve.wait_ge(nu_ready, c + 1)
                link(dve.tensor_tensor(og[:, c, :], n3[:, c, :], nu[:, c, :], ALU.mult))
                step(dve.tensor_reduce(amax["o"][:, c:c + 1], og[:, c, :], X, ALU.max,
                                       apply_absolute_value=True))
            max_over("o", IC)
            make_scale("o")
            link(dve.tensor_scalar(tscale[:, :], scale["o"][:, :], tg[:, G_FFN1:G_FFN1 + 1], None, ALU.mult))
            for n in range(IC * HALVES):
                c, h = n // HALVES, n % HALVES
                dve.wait_ge(n4_ready, n + 1)
                whole, hi = half(n4[:, c, :], h), half(o_hi[:, c, :], h)
                if h == 0:
                    link(dve.tensor_copy(hi, whole))
                else:
                    dve.wait_ge(ohi_ready, c + 1)
                dve.tensor_tensor(half(o_lo[:, c, :], h), whole, hi.bitcast(f32), ALU.subtract)\
                    .then_inc(olo_ready, 1)
            dve.wait_ge(x4T_ready, HALVES)
            for h in range(HALVES):
                dve.wait_ge(dn_mm, h + 1)
                dve.scalar_tensor_tensor(out=half(res, h), in0=bank[6 + h][:, :], scalar=tscale[:, :],
                                         in1=half(x4T, h), op0=ALU.mult, op1=ALU.add).then_inc(res_ready, 1)

        @block.tensor
        def _(pe):
            pe.sem_inc(z_ready, CREDIT)
            pe.sem_inc(y_done, CREDIT)
            mm = pe.matmul

            def keep_warm(b, n):
                for _ in range(n):
                    mm(bank[b][:, 0:256], zero16[:, 0:128], zero16[:, 0:256], start=True, stop=True)

            WARM_XN = {1: (5, 2), 2: (5, 2), 3: (0, 0), 4: (1, 16), 5: (7, 8), 6: (7, 8), 7: (1, 4), 8: (1, 6)}

            def transposes(dst, src, h, ident_=ident):
                for t in range(TILES):
                    last = pe.transpose(dst[:, t * 128:(t + 1) * 128], src[:, h * TILES + t, :], ident_[:, :])
                return last

            def normalised(dst, n):
                keep_warm(*WARM_XN[n])
                pe.wait_ge(xn_ready, n)
                pe.wait_ge(xn_act, n)
                transposes(dst, xn, (n - 1) % HALVES).then_inc(xT_mm, 1)

            def three(dst, whi, wlo, xh, xl, start, stop):
                mm(dst, whi, xh, start=start, stop=False)
                mm(dst, whi, xl, start=False, stop=False)
                return mm(dst, wlo, xh, start=False, stop=stop)

            def bias_rows(dst, k):
                for part in (row_hi, row_lo):
                    mm(dst[:, :], ones_r[:, :], part[:, k, :].unsqueeze(1).broadcast_to([1, TILES, D]),
                       start=(part is row_hi), stop=False)

            def context_rows(dst, w, bias):
                mm(dst, ones[0:1, 0:128], bias.unsqueeze(1).broadcast_to([1, HALVES, D]), start=True, stop=False)
                for h in range(HALVES):
                    last = mm(dst[:, h * D:(h + 1) * D], A("ctxT", 256)[:, h * 128:(h + 1) * 128], w,
                              start=False, stop=(h == HALVES - 1))
                return last

            def score_products(h):
                s = bank[h][:, 0:TILES * CTX]
                bias = bqk[0:1, h * BPH * CTX:(h + 1) * BPH * CTX]
                mm(s, ones[0:1, 0:128], bias.unsqueeze(1).broadcast_to([1, TPB, BPH * CTX]),
                   start=True, stop=False)
                pe.wait_ge(xT_ready, h + 1)
                for t in range(TILES):
                    b = h * BPH + t // TPB
                    slot = (t % TPB) * BPH + t // TPB
                    last = mm(s[:, slot * CTX:(slot + 1) * CTX], half(xT, h)[:, t * D:(t + 1) * D],
                              wqk[:, b * CTX:(b + 1) * CTX], start=False, stop=(t == TILES - 1))
                last.then_inc(s_mm, 1)

            def attend(h):
                pe.wait_ge(pr_ready, h + 1)
                for k in range(TPB):
                    last = pe.transpose(bank[2 + h][:, k * D:(k + 1) * D],
                                        sc[:, h, k * BPH:(k + 1) * BPH, :].rearrange("p b c -> p (b c)"),
                                        ident[:, :])
                last.then_inc(prT_mm, 1)
                keep_warm(5 + 2 * h, 3)
                pe.wait_ge(prT_ready, h + 1)
                for k in range(TPB):
                    for b in range(BPH):
                        rows_ = slice(b * CTX, (b + 1) * CTX)
                        last = mm(bank[4 + 2 * h + b][:, k * D:(k + 1) * D], prT[rows_, h, k, :], v0[rows_, h, :],
                                  start=True, stop=True)
                last.then_inc(pv_mm, 1)

            pe.wait_ge(zero_ready, 1)
            keep_warm(7, 15)
            pe.wait_ge(const_ready, 1)
            pe.wait_ge(row_in, 16)
            mm(bank[2][:, 0:4], ones[0:1, 0:128], R("g", 4), start=True, stop=True).then_inc(g_mm, 1)
            pe.wait_ge(pa_in, 16)
            mm(bank[0][:, 0:256], A("wkT", D), A("ctxT", 256), start=True, stop=True).then_inc(kT_mm, 1)
            keep_warm(7, 2)
            pe.wait_ge(kT_ready, 1)
            mm(bank[1][:, 0:256], A("wq", D), kT[:, :], start=True, stop=True)
            mm(bank[0][0:1, 0:256], A("bq", 1), kT[:, :], start=True, stop=True).then_inc(wqk_mm, 1)
            normalised(bank[6], 1)
            pe.wait_ge(wqk_ready, 1)
            score_products(0)
            normalised(bank[7], 2)
            context_rows(bank[3][:, 0:256], A("wvT", D), R("bv0")).then_inc(v0_mm, 1)
            score_products(1)
            pe.wait_ge(tg_ready, 1)
            pe.wait_ge(v0_ready, 1)
            attend(0)
            attend(1)
            pe.wait_ge(pb_in, 16)
            context_rows(bank[2][:, 0:256], B("wkT"), R("bk1"))
            context_rows(bank[2][:, 256:512], B("wvT"), R("bv1")).then_inc(kv1_mm, 1)
            for h in range(HALVES):
                pe.wait_ge(s_sub, h + 1)
                if h == 0:
                    keep_warm(0, 20)
                normalised(bank[h], 3 + h)

            def logits(h):
                pe.wait_ge(xlo_ready, h + 1)
                for t in range(TILES):
                    k = slice(h * HT + t * D, h * HT + (t + 1) * D)
                    at = t * EXPERTS
                    last = three(bank[2 + h][:, at:at + EXPERTS], xhi[:, k], xlo[:, k], rw_hi[:, :], rw_lo[:, :],
                                 True, True)
                last.then_inc(lg_mm, 1)

            def z_unit(u, j, e):
                odd, h, c = (j // 4) % 2, (j // 2) % 2, j % 2
                if j % 4 == 0:
                    pe.wait_ge(w1_split, e + 1)
                pe.wait_ge(gelu_done, CREDIT + u - NB + 1)
                k = slice(c * D, (c + 1) * D)
                three(bank[4 + j % NB][:, :], w_hi[odd][:, k], w_lo[odd][:, k], half(xhi, h), half(xlo, h),
                      True, True).then_inc(z_ready, 1)

            def gate_rows(k, e, h):
                pe.wait_ge(gated, CREDIT + FC * k - 2)
                lhsT = sel[:, :, :].rearrange("p e m -> p (e m)")[:, bass.ds(e * 128, 128)]
                mm(bank[2 + h][:, :], lhsT, half(gateT, h), start=True, stop=True).then_inc(gb_ready, 1)

            def y_unit(u, j, e, last):
                odd, h, c = (j // 4) % 2, (j // 2) % 2, j % 2
                if j % 4 == 0:
                    pe.wait_ge(w2_split, e + 1)
                pe.wait_ge(lo_done, CREDIT + u + 1)
                k = slice(256 + c * D, 256 + (c + 1) * D)
                b = j % NB
                three(bank[h][:, :], w_hi[odd][:, k], w_lo[odd][:, k], h_hi[b][:, :], h_lo[b][:, :],
                      False, last and j // 4 == 1 and c == 1).then_inc(y_done, 1)

            def units(i, last):
                for j in range(8):
                    if j % 2 == 0 and not (last and j == 6):
                        k = j // 2 + 1
                        gate_rows(4 * i + k, 2 * i + k // 2, k % 2)
                    if not (last and j >= 5):
                        z_unit(8 * i + j + 3, j + 3, 2 * i + (j + 3) // 4)
                    y_unit(8 * i + j, j, 2 * i + j // 4, last)

            pe.wait_ge(rw_ready, 1)
            pe.wait_ge(k1_ready, 1)
            logits(0)
            z_unit(0, 0, 0)
            z_unit(1, 1, 0)
            for h in range(HALVES):
                pe.wait_ge(xlo_ready, h + 1)
                mm(bank[h][:, :], zero16[:, 0:128], zero16[:, :], start=True, stop=False)
            logits(1)

            def gate_columns(h):
                pe.wait_ge(lg_read, h + 1)
                pe.wait_ge(gpart_ready, h + 1)
                transposes(bank[2 + h][:, 0:256].bitcast(f16), gpart, h, ident16).then_inc(gateT_mm, 1)

            gate_columns(0)
            z_unit(2, 2, 0)
            pe.wait_ge(gateT_ready, 1)
            gate_rows(0, 0, 0)
            keep_warm(7, 12)
            gate_columns(1)
            keep_warm(7, 6)
            pe.wait_ge(gateT_ready, 2)
            with pe.Fori(0, EXPERTS // 2 - 1) as i:
                units(i, False)
            units(EXPERTS // 2 - 1, True)

            for h in range(HALVES):
                pe.wait_ge(yT_ready, h + 1)
                for t in range(TILES):
                    last = pe.transpose(bank[4 + h][:, t * D:(t + 1) * D], half(yT, h)[:, t * D:(t + 1) * D],
                                        ident[:, :])
                last.then_inc(yN_mm, 1)
            pe.wait_ge(wb_ready, 1)
            for c in range(IC):
                if c >= 2:
                    keep_warm(6, 7)
                    pe.wait_ge(wT_ready, c - 1)
                for k in range(IC):
                    last = pe.transpose(bank[2 + c % 2][:, k * D:(k + 1) * D], wb_i[:, IC * c + k, :], ident[:, :])
                last.then_inc(wT_mm, 1)
            def key_products():
                pe.wait_ge(k1_soft, 3)
                for k in range(BPH):
                    rows_ = slice(k * CTX, (k + 1) * CTX)
                    for h in range(HALVES):
                        last = mm(bank[2 + k][:, h * (D + 1):(h + 1) * (D + 1)], k1[rows_, h, :], v1[rows_, h, :],
                                  start=True, stop=True)
                    last.then_inc(kv_mm, 1)

            for h in range(HALVES):
                bias_rows(bank[h], 0)
            keep_warm(6, 4)
            pe.wait_ge(wT_ready, IC)
            key_products()
            for h in range(HALVES):
                normalised(bank[6 + h], 5 + h)
                pe.wait_ge(xT_ready, 3 + h)
                for t in range(TILES):
                    last = mm(bank[h][:, t * D:(t + 1) * D], half(xT, h)[:, t * D:(t + 1) * D], B("wqT"),
                              start=False, stop=(t == TILES - 1))
                last.then_inc(q_mm, 1)
            pe.wait_ge(kv_raw_ready, BPH)
            for h in range(HALVES):
                bias_rows(bank[2 + h], 1)
            pe.wait_ge(x3_ready, HALVES)
            for h in range(HALVES):
                keep_warm(6, 4)
                pe.wait_ge(qe_ready, h + 1)
                for t in range(TILES):
                    last = pe.transpose(bank[4 + h][:, t * D:(t + 1) * D], qe[h][:, t * D:(t + 1) * D], ident[:, :])
                last.then_inc(qeT_mm, 1)
            pe.wait_ge(kv_ready, 1)
            for h in range(HALVES):
                if h == 0:
                    keep_warm(7, 3)
                pe.wait_ge(qeT_ready, h + 1)
                for t in range(TILES):
                    b = h * BPH + t // TPB
                    q = qeT[h][:, t * D:(t + 1) * D]
                    mm(bank[6 + h][:, t * D:(t + 1) * D], q, kv[:, b, :], start=True, stop=True)
                    last = mm(bank[h][:, t * 2 * HEADS:(t + 1) * 2 * HEADS], q,
                              kc[:, b, :, :].rearrange("p k a -> p (k a)"), start=True, stop=True)
                last.then_inc(nd_mm, 1)
            for h in range(HALVES):
                keep_warm(5, 12 if h == 0 else 4)
                pe.wait_ge(ao_ready, h + 1)
                for t in range(TILES):
                    last = pe.transpose(bank[4 + h][:, t * D:(t + 1) * D], ao[h][:, t * D:(t + 1) * D], ident[:, :])
                last.then_inc(aoT_mm, 1)
                keep_warm(5 - h, 3)
                pe.wait_ge(aoT_ready, h + 1)
                for t in range(TILES):
                    last = mm(bank[2 + h][:, t * D:(t + 1) * D], aoT[h][:, t * D:(t + 1) * D], B("wpT"),
                              start=False, stop=(t == TILES - 1))
                last.then_inc(proj_mm, 1)
            for h in range(HALVES):
                keep_warm(1, 3)
                pe.wait_ge(x4_ready, h + 1)
                transposes(bank[4 + h], x4, h).then_inc(x4T_mm, 1)
            for h in range(HALVES):
                normalised(bank[6 + h], 7 + h)

            keep_warm(1, 12)
            pe.wait_ge(wT_split, IC)
            pe.wait_ge(x4T_ready, HALVES)
            for n in range(2 * IC * HALVES):
                c, h = n // HALVES, n % HALVES
                w = c + IC if c < IC else c - IC
                if n < HALVES:
                    pe.wait_ge(nx_ready, h + 1)
                if n >= 6:
                    pe.wait_ge(gu_ready, n - 5)
                three(bank[n % 6][:, :], wT_hi[:, w, :], wT_lo[:, w, :], half(xhi, h), half(xlo, h),
                      True, True).then_inc(gu_mm, 1)
            pe.wait_ge(n3_ready, IC - 1)
            keep_warm(0, 16)
            pe.wait_ge(amax_ready["o"], 1)
            keep_warm(0, 10)
            for n in range(IC * HALVES):
                c, h = n // HALVES, n % HALVES
                pe.wait_ge(olo_ready, n + 1)
                last = three(bank[6 + h][:, :], wT_hi[:, 2 * IC + c, :], wT_lo[:, 2 * IC + c, :],
                             half(o_hi[:, c, :], h), half(o_lo[:, c, :], h), c == 0, c == IC - 1)
                if c == IC - 1:
                    last.then_inc(dn_mm, 1)


def kernel(**inputs):
    import concourse.bacc as _bacc
    from concourse import mybir as _mybir
    from concourse.bass_utils import run_bass_kernel_spmd as _run

    a = {k: np.asarray(v) for k, v in inputs.items()}

    def chunks(w):
        return w.reshape(-1, D, w.shape[1]).transpose(1, 0, 2)

    packa = np.concatenate([a["L0_xattn_Wq"], a["L0_xattn_Wk"].T, a["L0_xattn_Wv"].T,
                            a["ctx_1024"].reshape(BATCH * CTX, D).T, a["L0_ffn_router_w"].T,
                            a["L0_xattn_bq"][:, None], a["L0_xattn_bk"][:, None]], axis=1)
    packb = np.concatenate([a[f"L1_xattn_W{k}"].T for k in "qkvp"], axis=1)
    rows = np.concatenate([a["L0_xattn_bv"], a["L1_xattn_bq"], a["L1_xattn_bk"], a["L1_xattn_bv"],
                           a["L1_xattn_bp"], a["g_xattn"], a["g_ffn"]])[None]
    w1 = a["L0_ffn_w1"].transpose(2, 0, 1)
    w2 = a["L0_ffn_w2"].transpose(2, 0, 1).reshape(FC, D, EXPERTS, D).transpose(1, 2, 0, 3)
    experts = np.concatenate([w1, w2.reshape(D, EXPERTS, FC * D)], axis=2).reshape(D, -1)
    lpbq = np.concatenate([chunks(a["L1_ffn_w_up"]), chunks(a["L1_ffn_w_gate"]),
                           a["L1_ffn_w_down"].reshape(D, IC, D)], axis=1)
    arrays = {"in_x": a["x"], "in_packa": packa, "in_packb": packb, "in_rows": rows,
              "in_experts": experts, "in_lpbq": lpbq}
    arrays = {k: np.ascontiguousarray(v) for k, v in arrays.items()}
    nc = _bacc.Bacc("TRN2", target_bir_lowering=False, num_devices=1)
    args = [nc.dram_tensor(k, v.shape, _mybir.dt.from_np(v.dtype), kind="ExternalInput").ap()
            for k, v in arrays.items()]
    out = nc.dram_tensor("out", (D, TOKENS), _mybir.dt.float32, kind="ExternalOutput").ap()
    build(nc, *args, out)
    r = _run(nc, [arrays], core_ids=[0])
    return np.ascontiguousarray(r.results[0]["out"].T).reshape(BATCH, SEQ, D)
```

```python
import numpy as np

D = 128
BATCH, SEQ, CTX = 4, 256, 64
TOKENS = BATCH * SEQ
HALVES = 2
HT = TOKENS // HALVES
TILES = HT // D
BPH = BATCH // HALVES
TPB = SEQ // D
EXPERTS = 8
FC = 2
HEADS, HD = 16, 8
INTER = 384
IC = INTER // D
QBLOCK = 32
NBLK = D // QBLOCK
LN_EPS = 1e-5
QMAX = 32767.0
WQMAX = 7.0
QMIN_SCALE = 1e-12
SIG_STEPS = 65536.0
ROUND = 1.5 * 2.0 ** 23

PA = {"wq": 0, "wkT": 128, "wvT": 256, "ctxT": 384, "rwT": 640, "bq": 648, "bk": 649}
PA_COLS = 650
PB = {"wqT": 0, "wkT": 128, "wvT": 256, "wpT": 384}
PB_COLS = 512
ROW = {"bv0": 0, "bq1": 128, "bk1": 256, "bv1": 384, "bp1": 512, "g": 640}
ROW_COLS = 644
G_XATTN0, G_XATTN1, G_FFN0, G_FFN1 = 0, 1, 2, 3


def build(nc, x, packa, packb, rows, experts, lpbq, gates, out):
    import concourse.bass as bass
    from concourse import mybir
    from contextlib import ExitStack

    f32, f32r, f16 = mybir.dt.float32, mybir.dt.float32r, mybir.dt.float16
    i16, u16 = mybir.dt.int16, mybir.dt.uint16
    ACT = mybir.ActivationFunctionType
    ALU = mybir.AluOpType
    X = mybir.AxisListType.X

    ctx = ExitStack()
    with ctx:
        def sb(name, shape, dt=f32):
            return ctx.enter_context(nc.sbuf_tensor(name, shape, dt))

        def sem(name):
            return ctx.enter_context(nc.semaphore(name))

        bank = [ctx.enter_context(nc.psum_tensor(f"bank{i}", [128, 512], f32)) for i in range(8)]

        xin = sb("xin", [128, 8, D])
        pa = sb("pa", [128, PA_COLS])
        pb = sb("pb", [128, PB_COLS])
        row = sb("row", [1, ROW_COLS])
        ones_r = sb("ones_r", [1, 128], f32r)
        row_hi = sb("row_hi", [1, 2, D], f32r)
        row_lo = sb("row_lo", [1, 2, D], f32r)
        wexp = sb("wexp", [128, EXPERTS * 512])
        wq4 = sb("wq4", [128, 3 * IC, D])

        def A(name, n):
            return pa[:, PA[name]:PA[name] + n]

        def B(name):
            return pb[:, PB[name]:PB[name] + D]

        def R(name, n=D):
            return row[0:1, ROW[name]:ROW[name] + n]

        ident = sb("ident", [128, 128])
        ones = sb("ones", [128, 256])
        zero16 = sb("zero16", [128, 512], f16)
        head_mask = sb("head_mask", [128, HEADS, HD])
        number = sb("number", [128, EXPERTS])
        first_row = sb("first_row", [EXPERTS, 128])
        neg_half = sb("neg_half", [128, TILES])

        kT = sb("kT", [128, BATCH * CTX])
        wqk = sb("wqk", [128, BATCH * CTX])
        v0 = sb("v0", [128, HALVES, D])
        k1 = sb("k1", [128, HALVES, D])
        k1e = sb("k1e", [128, HALVES, D])
        v1 = sb("v1", [128, HALVES, D + 1])
        k1max = sb("k1max", [128, HALVES * HEADS])
        k1sum = sb("k1sum", [128, HALVES * HEADS])
        kv_raw = sb("kv_raw", [128, BPH, HALVES, D + 1])
        NUM, DEN = D, 2 * HEADS
        kv = sb("kv", [128, BATCH, NUM + DEN])
        tg = sb("tg", [128, 4])

        stats = sb("stats", [128, HALVES, TILES, 6])
        mv = sb("mv", [128, HALVES, TILES, 2])
        var = sb("var", [128, HALVES, TILES])
        rstd = sb("rstd", [128, HALVES, TILES])
        shift = sb("shift", [128, HALVES, TILES])
        xn = sb("xn", [128, 8, D])
        xT = sb("xT", [128, TOKENS])
        xhi = sb("xhi", [128, TOKENS], f32r)
        xlo = sb("xlo", [128, TOKENS], f32r)
        smax = sb("smax", [128, HALVES, TILES])
        ssum = sb("ssum", [128, HALVES, TILES])
        sc = sb("sc", [128, HALVES, TILES, CTX])
        prT = sb("prT", [128, HALVES, TPB, D])
        x2 = sb("x2", [128, 8, D])
        rw_hi = sb("rw_hi", [128, EXPERTS], f32r)
        rw_lo = sb("rw_lo", [128, EXPERTS], f32r)
        NT = HALVES * TILES
        lg_ = sb("lg", [128, NT, EXPERTS])
        best_ = sb("best", [128, NT, EXPERTS])
        place_ = sb("place", [128, NT, EXPERTS], mybir.dt.uint32)
        top1_ = sb("top1", [128, NT, EXPERTS])
        top2_ = sb("top2", [128, NT, EXPERTS])
        gate_ = sb("gate", [128, NT, EXPERTS])
        g1_ = sb("g1", [128, HALVES, TILES])
        g2_ = sb("g2", [128, HALVES, TILES])
        mr_ = sb("mr", [128, HALVES, TILES])
        ex_ = sb("ex", [128, HALVES, TILES])
        gateT = sb("gateT", [EXPERTS, TOKENS])
        NB = 4
        high_parts = sb("high_parts", [128, 6 * 512], f32r)
        low_parts = sb("low_parts", [128, 6 * 512], f32r)
        hidden = sb("hidden", [128, 2 * NB * 512])

        def buffers(t, start, n):
            return [t[:, k * 512:(k + 1) * 512] for k in range(start, start + n)]

        h_hi, w_hi = buffers(high_parts, 0, NB), buffers(high_parts, NB, 2)
        h_lo, w_lo = buffers(low_parts, 0, NB), buffers(low_parts, NB, 2)
        ge, hm = buffers(hidden, 0, NB), buffers(hidden, NB, NB)
        yT = xT
        x3 = sb("x3", [128, 8, D])
        qe, qn, qmax, inv, qeT, ao, aoT = [], [], [], [], [], [], []
        q_exp, q_soft = sb("q_exp", [128, TOKENS]), sb("q_soft", [128, TOKENS])
        gate_rows = (q_exp, q_soft)
        for h in range(HALVES):
            qe.append(q_exp[:, h * HT:(h + 1) * HT])
            qn.append(q_soft[:, h * HT:(h + 1) * HT])
            qmax.append(sb(f"qmax{h}", [128, TILES * HEADS]))
            inv.append(sb(f"inv{h}", [128, TILES, 2, HEADS]))
            qeT.append(hidden[:, h * 512:(h + 1) * 512])
            ao.append(hidden[:, (2 + h) * 512:(3 + h) * 512])
            aoT.append(hidden[:, (4 + h) * 512:(5 + h) * 512])
        x4 = sb("x4", [128, 8, D])
        x4T = sb("x4T", [128, TOKENS])
        wb_max = sb("wb_max", [128, 3 * IC * NBLK])
        wb_s = sb("wb_s", [128, 3 * IC * NBLK])
        wb_r = sb("wb_r", [128, 3 * IC * NBLK])
        wb_i = sb("wb_i", [128, 3 * IC, D])
        wT = sb("wT", [128, 3 * IC, D])
        wT_hi = sb("wT_hi", [128, 3 * IC, D], f32r)
        wT_lo = sb("wT_lo", [128, 3 * IC, D], f32r)
        nx = sb("nx", [128, TOKENS], i16)
        gq = sb("gq", [128, IC, TOKENS])
        ng = sb("ng", [128, IC, TOKENS], i16)
        def third(t, dt=None):
            t = t if dt is None else t.bitcast(dt)
            return t.rearrange("p (c n) -> p c n", c=IC)

        nu = third(wexp[:, 0:1536], i16)
        sq = third(wexp[:, 1536:3072], u16)
        sg = third(hidden[:, 0:3072])
        pg = sg
        n3 = ng
        og = gq
        n4 = nu
        o_hi = third(high_parts[:, :])
        o_lo = third(low_parts[:, :])
        res = hidden[:, 3072:4096]
        STG = ("x", "g", "u", "p", "o")
        amax = {k: sb(f"amax_{k}", [128, 6]) for k in STG}
        amax1 = {k: sb(f"amax1_{k}", [128, 1]) for k in STG}
        gmax = {k: sb(f"gmax_{k}", [128, 1]) for k in STG}
        scale = {k: sb(f"scale_{k}", [128, 1]) for k in STG}
        step_raw = {k: sb(f"step_raw_{k}", [128, 1]) for k in STG}
        mul = {k: sb(f"mul_{k}", [128, 1]) for k in STG}
        unit = {k: sb(f"unit_{k}", [128, 1]) for k in "po"}
        per_unit = {k: sb(f"per_unit_{k}", [128, 1]) for k in "po"}
        unit["g"] = unit["u"] = scale["x"]
        per_unit["g"] = per_unit["u"] = mul["x"]
        per_scale = {k: sb(f"per_scale_{k}", [128, 1]) for k in "gup"}
        floor = {k: sb(f"floor_{k}", [128, 1]) for k in "gpo"}
        floor["u"] = floor["g"]
        tscale = sb("tscale", [128, 1])
        table_load = sb("table_load", [1, 2])

        x_in = [sem(f"x_in{h}") for h in range(HALVES)]
        pa_in, pb_in, row_in, exp_in, lpbq_in, out_done = map(
            sem, ("pa_in", "pb_in", "row_in", "exp_in", "lpbq_in", "out_done"))
        const_ready, const_late, pool_step = map(sem, ("const_ready", "const_late", "pool_step"))
        dve_step, zero_ready = map(sem, ("dve_step", "zero_ready"))
        kT_mm, kT_ready, v0_mm, v0_ready, g_mm, tg_ready = map(
            sem, ("kT_mm", "kT_ready", "v0_mm", "v0_ready", "g_mm", "tg_ready"))
        wqk_mm, wqk_ready, kv1_mm, k1_ready, k1_soft = map(
            sem, ("wqk_mm", "wqk_ready", "kv1_mm", "k1_ready", "k1_soft"))
        kv_mm, kv_raw_ready, kv_ready = map(sem, ("kv_mm", "kv_raw_ready", "kv_ready"))
        var_ready, rstd_ready, xn_ready, xT_mm, xT_ready = map(
            sem, ("var_ready", "rstd_ready", "xn_ready", "xT_mm", "xT_ready"))
        s_mm, s_sub, shift_ready, xn_act, pr_ready, prT_mm, prT_ready, pv_mm = map(
            sem, ("s_mm", "s_sub", "shift_ready", "xn_act", "pr_ready", "prT_mm", "prT_ready", "pv_mm"))
        xhi_ready, xlo_ready, rw_ready, lg_mm, lg_read, dm_ready, ex_ready = map(
            sem, ("xhi_ready", "xlo_ready", "rw_ready", "lg_mm", "lg_read", "dm_ready", "ex_ready"))
        gate_ready, gateT_mm = map(sem, ("gate_ready", "gateT_mm"))
        gateT_ready = [sem(f"gateT_ready{h}") for h in range(HALVES)]
        gates_out, first_rows_mm = map(sem, ("gates_out", "first_rows_mm"))
        rows_in = [sem(f"rows_in{odd}") for odd in range(2)]
        w1_split, w2_split, z_ready = map(sem, ("w1_split", "w2_split", "z_ready"))
        gelu_done, gated, hi_done, lo_done, y_done = map(
            sem, ("gelu_done", "gated", "hi_done", "lo_done", "y_done"))
        yT_ready, yN_mm, x3_ready = map(sem, ("yT_ready", "yN_mm", "x3_ready"))
        q_mm, q_sub, qe_ready, qeT_mm, qeT_ready, inv_ready, qn_ready = map(
            sem, ("q_mm", "q_sub", "qe_ready", "qeT_mm", "qeT_ready", "inv_ready", "qn_ready"))
        nd_mm, ao_ready, aoT_mm, aoT_ready, proj_mm, x4_ready = map(
            sem, ("nd_mm", "ao_ready", "aoT_mm", "aoT_ready", "proj_mm", "x4_ready"))
        x4T_mm, x4T_ready, wb_scale, wb_ready, wT_mm, wT_ready, wT_split = map(
            sem, ("x4T_mm", "x4T_ready", "wb_scale", "wb_ready", "wT_mm", "wT_ready", "wT_split"))
        amax_ready = {k: sem(f"amax_ready_{k}") for k in STG}
        gmax_ready = {k: sem(f"gmax_ready_{k}") for k in STG}
        mul_ready = {k: sem(f"mul_ready_{k}") for k in STG}
        nx_ready, xq_ready, gu_mm, gu_ready, n3_ready = map(
            sem, ("nx_ready", "xq_ready", "gu_mm", "gu_ready", "n3_ready"))
        ng_ready, sg_ready, sq_ready, nu_ready, n4_ready, ohi_ready, olo_ready = map(
            sem, ("ng_ready", "sg_ready", "sq_ready", "nu_ready", "n4_ready", "ohi_ready", "olo_ready"))
        dn_mm, res_ready, nx_high, ohi_dve, scale_ready = map(
            sem, ("dn_mm", "res_ready", "nx_high", "ohi_dve", "scale_ready"))

        CREDIT = 8

        def nd_bank(h, k):
            return bank[6 + h] if k == 0 else bank[h]

        def half(t, h):
            return t[:, h * HT:(h + 1) * HT]

        def tiles(t, h):
            return t[:, h * TILES:(h + 1) * TILES, :]

        def by_head(t):
            return t[:, :].rearrange("p (a c) -> p a c", c=HD)

        block = ctx.enter_context(nc.Block())

        @block.sync
        def _(sp):
            xv = x.rearrange("b (t p) d -> p (b t) d", p=128)
            sp.dma_start(xin[:, 0:TILES, :], xv[:, 0:TILES, :]).then_inc(x_in[0], 16)
            sp.dma_start(pa[:, :], packa).then_inc(pa_in, 16)
            sp.dma_start(xin[:, TILES:, :], xv[:, TILES:, :]).then_inc(x_in[1], 16)
            sp.dma_start(pb[:, :], packb).then_inc(pb_in, 16)
            sp.dma_start(wq4[:, :, :], lpbq).then_inc(lpbq_in, 16)
            sp.dma_start(wexp[:, :], experts).then_inc(exp_in, 16)
            for h in range(HALVES):
                sp.wait_ge(gateT_ready[h], 1)
            sp.dma_start(gates[:, :], gateT[:, :]).then_inc(gates_out, 16)
            sp.wait_ge(gates_out, 16)
            for e in range(1, EXPERTS):
                if e >= 2:
                    sp.wait_ge(gated, CREDIT + (e - 1) * HALVES * FC)
                sp.dma_start(gate_rows[e % 2][:, :], gates[e:e + 1, :].broadcast_to([128, TOKENS]))\
                    .then_inc(rows_in[e % 2], 16)
            for h in range(HALVES):
                sp.wait_ge(res_ready, h + 1)
                sp.dma_start(half(out, h), half(res, h)).then_inc(out_done, 16)
            sp.wait_ge(out_done, 16 * HALVES)

        @block.gpsimd
        def _(pool):
            steps = [0]

            def step(ins):
                steps[0] += 1
                ins.then_inc(pool_step, 1)
                return steps[0]

            def link(ins):
                pool.wait_ge(pool_step, step(ins))

            def rstd_of(n):
                pool.wait_ge(var_ready, n)
                h = (n - 1) % HALVES
                pool.tensor_tensor(rstd[:, h, :], var[:, h, :], neg_half[:, :], ALU.pow).then_inc(rstd_ready, 1)

            pool.memset(ident[:, :], 0.0)
            pool.memset(ones[:, :], 1.0)
            link(pool.memset(neg_half[:, :], -0.5))
            link(pool.affine_select(out=ident[:, :], in_=ident[:, :], compare_op=ALU.not_equal, fill=1.0,
                                    base=0, pattern=[[-1, 128]], channel_multiplier=1))
            pool.drain().then_inc(const_ready, 1)
            pool.memset(v1[:, :, D:D + 1], 1.0)
            pool.iota(number[:, :], pattern=[[1, EXPERTS]], base=0, channel_multiplier=0,
                      allow_small_or_imprecise_dtypes=True)
            rstd_of(1)
            rstd_of(2)
            link(pool.memset(first_row[:, :], 0.0))
            pool.memset(first_row[0:1, :], 1.0)
            link(pool.memset(head_mask[:, :, :], 1.0))
            link(pool.affine_select(out=head_mask[:, :, :], in_=head_mask[:, :, :], compare_op=ALU.is_ge,
                                    fill=0.0, base=0, pattern=[[-HD, HEADS], [0, HD]],
                                    channel_multiplier=1))
            link(pool.affine_select(out=head_mask[:, :, :], in_=head_mask[:, :, :], compare_op=ALU.is_ge,
                                    fill=0.0, base=HD - 1, pattern=[[HD, HEADS], [0, HD]],
                                    channel_multiplier=-1))
            for b in range(BATCH):
                pool.tensor_tensor(kv[:, b, D + HEADS:], head_mask[:, :, 0], head_mask[:, :, 0], ALU.mult)
            pool.wait_ge(row_in, 16)
            pool.tensor_tensor(ones_r[:, :], ones[0:1, 0:128], ones[0:1, 0:128], ALU.mult)
            for k, name in enumerate(("bq1", "bp1")):
                link(pool.tensor_tensor(row_hi[:, k, :], R(name), ones[0:1, 0:128], ALU.mult))
                pool.tensor_tensor(row_lo[:, k, :], R(name), row_hi[:, k, :].bitcast(f32), ALU.subtract)
            pool.drain().then_inc(const_late, 1)
            rstd_of(3)
            rstd_of(4)

            def split_pair(i):
                for odd in range(2):
                    e = 2 * i + odd
                    for w2, (free, done) in enumerate(((z_ready, w1_split), (y_done, w2_split))):
                        pool.wait_ge(free, CREDIT + 4 * e - 4)
                        cols = 256 * w2
                        raw = wexp[:, bass.ds(e * 512 + cols, 256)]
                        hi, lo = w_hi[odd][:, cols:cols + 256], w_lo[odd][:, cols:cols + 256]
                        pool.tensor_tensor(hi, raw, ones[:, 0:256], ALU.mult)
                        pool.drain()
                        pool.tensor_tensor(lo, raw, hi.bitcast(f32), ALU.subtract).then_inc(done, 1)

            pool.wait_ge(exp_in, 16)
            split_pair(0)

            pool.wait_ge(wb_scale, 1)
            blocks = wq4[:, :, :].rearrange("p c (b k) -> p (c b) k", k=QBLOCK)
            shape = [128, 3 * IC * NBLK, QBLOCK]
            ints = wb_i[:, :, :].rearrange("p c (b k) -> p (c b) k", k=QBLOCK)
            link(pool.tensor_tensor(ints, blocks, wb_r[:, :].unsqueeze(2).broadcast_to(shape), ALU.mult))
            with pool.Fori(1, EXPERTS // 2) as i:
                split_pair(i)
            link(pool.tensor_scalar(wb_i[:, :, :], wb_i[:, :, :], ROUND, -ROUND, ALU.add, ALU.add))
            pool.tensor_tensor(ints, ints, wb_s[:, :].unsqueeze(2).broadcast_to(shape), ALU.mult)\
                .then_inc(wb_ready, 1)
            rstd_of(5)
            rstd_of(6)
            mask = head_mask[:, :, 0]
            for k in range(BPH):
                pool.wait_ge(kv_raw_ready, k + 1)
                for h in range(HALVES):
                    b = h * BPH + k
                    pool.tensor_tensor(kv[:, b, 0:D], kv_raw[:, k, h, 0:D],
                                       head_mask[:, :, :].rearrange("p a b -> p (a b)"), ALU.mult)
                    pool.tensor_tensor(kv[:, b, D:D + HEADS], kv_raw[:, k, h, D:D + 1].broadcast_to([128, HEADS]), mask,
                                       ALU.mult)
            pool.drain().then_inc(kv_ready, 1)
            for c in range(IC):
                pool.wait_ge(wT_ready, c + 1)
                k = slice(IC * c, IC * c + IC)
                pool.tensor_tensor(wT_lo[:, k, :], wT[:, k, :], wT_hi[:, k, :].bitcast(f32), ALU.subtract)\
                    .then_inc(wT_split, 1)
            for h in range(HALVES):
                r = inv[h][:, :, 1, :]
                for t in range(TILES):
                    pool.wait_ge(inv_ready, h * BPH + t // TPB + 1)
                    last = pool.tensor_tensor(by_head(qn[h])[:, t * HEADS:(t + 1) * HEADS, :],
                                              by_head(qe[h])[:, t * HEADS:(t + 1) * HEADS, :],
                                              r[:, t, :].unsqueeze(2).broadcast_to([128, HEADS, HD]), ALU.mult)
                last.then_inc(qn_ready, 1)
            rstd_of(7)
            rstd_of(8)
            for k in STG:
                pool.wait_ge(amax_ready[k], 1)
                pool.partition_all_reduce(gmax[k][:, :], amax1[k][:, :], 128, bass.bass_isa.ReduceOp.absmax)\
                    .then_inc(gmax_ready[k], 1)

        @block.scalar
        def _(act):
            act.sem_inc(gelu_done, CREDIT)
            act.sem_inc(hi_done, CREDIT)

            def evac(dst, src, ready, n, done):
                act.wait_ge(ready, n)
                act.activation(dst, src, ACT.Copy).then_inc(done, 1)

            def normalise(src, n):
                h = (n - 1) % HALVES
                if n > 2:
                    act.wait_ge(xT_mm, n - 2)
                act.wait_ge(shift_ready, n)
                for t in range(TILES // 2, TILES):
                    last = act.activation(xn[:, h * TILES + t, :], src[:, h * TILES + t, :], ACT.Identity,
                                          bias=shift[:, h, t:t + 1], scale=rstd[:, h, t:t + 1])
                last.then_inc(xn_act, 1)

            act.dma_start(row[:, :], rows).then_inc(row_in, 16)
            act.wait_ge(g_mm, 1)
            act.activation(tg[:, :], bank[2][:, 0:4], ACT.Tanh).then_inc(tg_ready, 1)
            act.wait_ge(kT_mm, 1)
            act.activation(kT[:, :], bank[0][:, 0:256], ACT.Identity, bias=A("bk", 1)).then_inc(kT_ready, 1)
            normalise(xin, 1)
            act.wait_ge(wqk_mm, 1)
            act.activation(wqk[:, :], bank[5][:, 0:256], ACT.Copy).then_inc(wqk_ready, 1)
            evac(half(xT, 0), bank[6][:, :], xT_mm, 1, xT_ready)
            normalise(xin, 2)
            evac(half(xT, 1), bank[7][:, :], xT_mm, 2, xT_ready)
            for h in range(HALVES):
                act.wait_ge(s_sub, h + 1)
                act.activation(sc[:, h, :, :], sc[:, h, :, :], ACT.Exp).then_inc(pr_ready, 1)
                if h == 0:
                    evac(v0[:, :, :].rearrange("p b d -> p (b d)"), bank[3][:, 0:256], v0_mm, 1, v0_ready)
                evac(prT[:, h, :, :].rearrange("p t d -> p (t d)"), bank[2 + h][:, 0:256],
                     prT_mm, h + 1, prT_ready)
            act.wait_ge(kv1_mm, 1)
            act.activation(k1[:, :, :].rearrange("p b d -> p (b d)"), bank[2][:, 0:256], ACT.Copy)
            act.activation(v1[:, :, 0:D], bank[2][:, 256:512].rearrange("p (h d) -> p h d", d=D), ACT.Copy)\
                .then_inc(k1_ready, 1)
            for h in range(HALVES):
                normalise(x2, 3 + h)
                evac(half(xhi, h), bank[h][:, :], xT_mm, 3 + h, xhi_ready)
            act.wait_ge(k1_soft, 1)
            act.activation(k1e[:, :, :], k1[:, :, :], ACT.Exp).then_inc(k1_soft, 1)

            for h in range(HALVES):
                act.wait_ge(dm_ready, h + 1)
                act.activation(ex_[:, h, :], g2_[:, h, :], ACT.Exp).then_inc(ex_ready, 1)
            act.wait_ge(gateT_mm, 1)
            act.activation(half(gateT, 0), bank[2][0:EXPERTS, :], ACT.Copy).then_inc(gateT_ready[0], 1)

            def gelu(u, j):
                act.wait_ge(z_ready, CREDIT + u + 1)
                act.wait_ge(gated, CREDIT + u - NB + 1)
                act.activation(ge[j % NB][:, :], bank[4 + j % NB][:, :], ACT.Gelu).then_inc(gelu_done, 1)

            def high(u, j):
                act.wait_ge(gated, CREDIT + u + 1)
                act.wait_ge(y_done, CREDIT + u - NB + 1)
                act.activation(h_hi[j % NB][:, :], hm[j % NB][:, :], ACT.Copy).then_inc(hi_done, 1)

            def units(i, last):
                for j in range(8):
                    if not (last and j == 7):
                        gelu(8 * i + j + 1, j + 1)
                    high(8 * i + j, j)

            gelu(0, 0)
            act.wait_ge(first_rows_mm, 1)
            act.activation(half(gate_rows[0], 0), bank[2][:, :], ACT.Copy).then_inc(rows_in[0], 8)
            with act.Fori(0, EXPERTS // 2 - 1) as i:
                units(i, False)
            units(EXPERTS // 2 - 1, True)

            evac(half(yT, 0), bank[0][:, :], y_done, CREDIT + 30, yT_ready)
            act.activation(table_load[:, 1:2], row[0:1, 0:1], ACT.Exp)
            evac(half(yT, 1), bank[1][:, :], y_done, CREDIT + 32, yT_ready)
            for c in range(IC):
                act.wait_ge(wT_mm, c + 1)
                src = bank[2 + c % 2][:, 0:IC * D].rearrange("p (c d) -> p c d", d=D)
                k = slice(IC * c, IC * c + IC)
                act.activation(wT_hi[:, k, :], src, ACT.Copy)
                act.activation(wT[:, k, :], src, ACT.Copy).then_inc(wT_ready, 1)
            for h in range(HALVES):
                normalise(x3, 5 + h)
                evac(half(xT, h), bank[6 + h][:, :], xT_mm, 5 + h, xT_ready)
            for h in range(HALVES):
                act.wait_ge(q_sub, h + 1)
                act.activation(qe[h][:, :], qe[h][:, :], ACT.Exp).then_inc(qe_ready, 1)
                evac(qeT[h], bank[4 + h][:, :], qeT_mm, h + 1, qeT_ready)
            for h in range(HALVES):
                evac(aoT[h], bank[4 + h][:, :], aoT_mm, h + 1, aoT_ready)
            act.activation(table_load[:, 0:1], row[0:1, 0:1], ACT.Sigmoid)
            for h in range(HALVES):
                normalise(x4, 7 + h)
            for h in range(HALVES):
                evac(half(x4T, h), bank[4 + h][:, :], x4T_mm, h + 1, x4T_ready)
            act.wait_ge(mul_ready["x"], 1)
            for h in range(HALVES):
                act.wait_ge(xT_mm, 7 + h)
                act.activation(half(nx, h), bank[6 + h][:, :], ACT.Copy, scale=mul["x"][:, :]).then_inc(xq_ready, 1)

            for n in range(IC * HALVES):
                act.wait_ge(gu_mm, n + 1)
                act.activation(half(gq[:, n // HALVES, :], n % HALVES), bank[n][:, :], ACT.Copy)\
                    .then_inc(gu_ready, 1)

            act.wait_ge(mul_ready["g"], 1)
            for c in range(IC):
                act.activation(ng[:, c, :], gq[:, c, :], ACT.Copy, scale=mul["g"][:, :]).then_inc(ng_ready, 1)
                act.wait_ge(ng_ready, c + 1)
                act.wait_ge(scale_ready, 1)
                act.activation(sg[:, c, :], ng[:, c, :], ACT.Sigmoid, scale=scale["g"][:, :])\
                    .then_inc(sg_ready, 1)
                if c > 0:
                    act.wait_ge(sg_ready, c + 1)
                    act.activation(sq[:, c, :], sg[:, c, :], ACT.Copy, scale=SIG_STEPS).then_inc(sq_ready, 1)
            act.wait_ge(mul_ready["u"], 1)
            for n in range(IC * HALVES):
                act.activation(half(nu[:, n // HALVES, :], n % HALVES), bank[n][:, :], ACT.Copy,
                               scale=mul["u"][:, :]).then_inc(nu_ready, 1)
            act.wait_ge(mul_ready["p"], 1)
            for c in range(1, IC):
                act.activation(n3[:, c, :], pg[:, c, :], ACT.Copy, scale=mul["p"][:, :]).then_inc(n3_ready, 1)
            act.wait_ge(mul_ready["o"], 1)
            for n in range(1, IC * HALVES):
                c, h = n // HALVES, n % HALVES
                act.activation(half(n4[:, c, :], h), half(og[:, c, :], h), ACT.Copy, scale=mul["o"][:, :])\
                    .then_inc(n4_ready, 1)
                if h == 1:
                    act.wait_ge(n4_ready, n)
                    act.activation(half(o_hi[:, c, :], h), half(n4[:, c, :], h), ACT.Copy).then_inc(ohi_ready, 1)

        @block.vector
        def _(dve):
            steps = [0]

            def step(ins):
                steps[0] += 1
                ins.then_inc(dve_step, 1)
                return steps[0]

            def link(ins):
                dve.wait_ge(dve_step, step(ins))

            dve.memset(zero16[:, :], 0.0).then_inc(zero_ready, 1)
            dve.sem_inc(gated, CREDIT)
            dve.sem_inc(lo_done, CREDIT)

            def statistics(src, h):
                for t in range(TILES):
                    m = step(dve.bn_stats(stats[:, h, t, :], src[:, h * TILES + t, :]))
                dve.wait_ge(dve_step, m)
                for t in range(TILES):
                    m = step(dve.bn_aggr(mv[:, h, t, :], stats[:, h, t, :]))
                dve.wait_ge(dve_step, m)
                dve.tensor_scalar(var[:, h, :], mv[:, h, :, 1], LN_EPS, None, ALU.add).then_inc(var_ready, 1)

            def normalise(src, n):
                h = (n - 1) % HALVES
                dve.wait_ge(rstd_ready, n)
                dve.scalar_tensor_tensor(out=shift[:, h, :], in0=mv[:, h, :, 0], scalar=-1.0,
                                         in1=rstd[:, h, :], op0=ALU.mult, op1=ALU.mult).then_inc(shift_ready, 1)
                if n > 2:
                    dve.wait_ge(xT_mm, n - 2)
                for t in range(TILES // 2):
                    last = dve.tensor_scalar(xn[:, h * TILES + t, :], src[:, h * TILES + t, :],
                                             mv[:, h, t, 0:1], rstd[:, h, t:t + 1], ALU.subtract, ALU.mult)
                last.then_inc(xn_ready, 1)

            def weight_scales():
                dve.wait_ge(lpbq_in, 16)
                link(dve.tensor_reduce(wb_max[:, :], wq4[:, :, :].rearrange("p c (b k) -> p (c b) k", k=QBLOCK),
                                       X, ALU.max, apply_absolute_value=True))
                link(dve.tensor_scalar(wb_s[:, :], wb_max[:, :], 1.0 / WQMAX, QMIN_SCALE, ALU.mult, ALU.max))
                dve.reciprocal(wb_r[:, :], wb_s[:, :]).then_inc(wb_scale, 1)

            def scores(h):
                s = bank[h][:, 0:TILES * CTX].rearrange("p (t c) -> p t c", c=CTX)
                dve.wait_ge(s_mm, h + 1)
                link(dve.tensor_reduce(smax[:, h, :], s, X, ALU.max))
                dve.tensor_tensor(sc[:, h, :, :], s, smax[:, h, :].unsqueeze(2).broadcast_to([128, TILES, CTX]),
                                  ALU.subtract).then_inc(s_sub, 1)

            def add_attention(h):
                dve.wait_ge(pr_ready, h + 1)
                link(dve.tensor_reduce(ssum[:, h, :], sc[:, h, :, :], X, ALU.add))
                link(dve.reciprocal(smax[:, h, :], ssum[:, h, :]))
                link(dve.tensor_scalar(ssum[:, h, :], smax[:, h, :], tg[:, G_XATTN0:G_XATTN0 + 1], None, ALU.mult))
                dve.wait_ge(pv_mm, h + 1)
                for t in range(TILES):
                    b, k = t // TPB, t % TPB
                    slot = k * BPH + b
                    last = dve.scalar_tensor_tensor(out=x2[:, h * TILES + t, :],
                                                    in0=bank[4 + 2 * h + b][:, k * D:(k + 1) * D],
                                                    scalar=ssum[:, h, slot:slot + 1],
                                                    in1=xin[:, h * TILES + t, :], op0=ALU.mult, op1=ALU.add)
                link(last)

            def low_tokens(h):
                dve.wait_ge(xhi_ready, h + 1)
                dve.tensor_tensor(half(xlo, h), bank[h][:, :], half(xhi, h).bitcast(f32), ALU.subtract)\
                    .then_inc(xlo_ready, 1)

            def route(h):
                wide = [128, TILES, EXPERTS]
                lg, best, place, top1, top2, gate = (tiles(t, h) for t in (lg_, best_, place_, top1_, top2_, gate_))
                mr, g1, g2, ex = (t[:, h, :] for t in (mr_, g1_, g2_, ex_))

                def over(t):
                    return t.broadcast_to(wide)

                order = number[:, :].unsqueeze(1).broadcast_to(wide)
                dve.wait_ge(const_late, 1)
                dve.wait_ge(lg_mm, h + 1)
                dve.tensor_copy(lg, bank[2 + h][:, 0:TILES * EXPERTS].rearrange("p (t e) -> p t e", e=EXPERTS))\
                    .then_inc(lg_read, 1)
                dve.wait_ge(lg_read, h + 1)
                for t in range(TILES):
                    n = step(dve.max(best[:, t, :], lg[:, t, :]))
                dve.wait_ge(dve_step, n)
                dve.tensor_tensor(g2, best[:, :, 1], best[:, :, 0], ALU.subtract).then_inc(dm_ready, 1)
                for t in range(TILES):
                    n = step(dve.max_index(place[:, t, :], best[:, t, :], lg[:, t, :]))
                dve.wait_ge(dve_step, n)
                dve.tensor_tensor(top1, order, over(place[:, :, 0:1]), ALU.is_equal)
                step(dve.tensor_tensor(top2, order, over(place[:, :, 1:2]), ALU.is_equal))
                dve.wait_ge(ex_ready, h + 1)
                m = step(dve.tensor_scalar(mr, ex, 1.0, None, ALU.add))
                dve.wait_ge(dve_step, m - 1)
                n = step(dve.tensor_tensor(top2, top2, over(ex.unsqueeze(2)), ALU.mult))
                dve.wait_ge(dve_step, m)
                m = step(dve.reciprocal(g1, mr))
                dve.wait_ge(dve_step, n)
                step(dve.tensor_tensor(top1, top1, top2, ALU.add))
                dve.wait_ge(dve_step, m + 1)
                dve.tensor_tensor(gate, top1, over(g1.unsqueeze(2)), ALU.mult).then_inc(gate_ready, 1)

            def keys_by_head(t):
                return t[:, :, :].rearrange("p b (a c) -> p (b a) c", c=HD)

            kwide = [128, HALVES * HEADS, HD]

            def keys_less_max():
                dve.wait_ge(k1_ready, 1)
                link(dve.tensor_reduce(k1max[:, :], keys_by_head(k1), X, ALU.max))
                dve.tensor_tensor(keys_by_head(k1), keys_by_head(k1),
                                  k1max[:, :].unsqueeze(2).broadcast_to(kwide), ALU.subtract).then_inc(k1_soft, 1)

            def keys_sum():
                dve.wait_ge(k1_soft, 2)
                step(dve.tensor_reduce(k1sum[:, :], keys_by_head(k1e), X, ALU.add))

            def keys_softmax(n):
                dve.wait_ge(dve_step, n)
                link(dve.reciprocal(k1max[:, :], k1sum[:, :]))
                dve.tensor_tensor(keys_by_head(k1), keys_by_head(k1e),
                                  k1max[:, :].unsqueeze(2).broadcast_to(kwide), ALU.mult).then_inc(k1_soft, 1)

            for h in range(HALVES):
                dve.wait_ge(x_in[h], 16)
                statistics(xin, h)
            normalise(xin, 1)
            normalise(xin, 2)
            dve.wait_ge(pa_in, 16)
            link(dve.tensor_copy(rw_hi[:, :], A("rwT", EXPERTS)))
            dve.tensor_tensor(rw_lo[:, :], A("rwT", EXPERTS), rw_hi[:, :].bitcast(f32), ALU.subtract)\
                .then_inc(rw_ready, 1)
            weight_scales()
            dve.wait_ge(tg_ready, 1)
            scores(0)
            scores(1)
            add_attention(0)
            statistics(x2, 0)
            add_attention(1)
            normalise(x2, 3)
            statistics(x2, 1)
            low_tokens(0)
            normalise(x2, 4)
            keys_less_max()
            low_tokens(1)
            route(0)
            route(1)
            keys_sum()
            n = steps[0]
            dve.wait_ge(gateT_mm, 2)
            dve.tensor_copy(half(gateT, 1), bank[3][0:EXPERTS, :]).then_inc(gateT_ready[1], 1)
            keys_softmax(n)

            def gate_unit(i, j):
                u = 8 * i + j
                dve.wait_ge(gelu_done, CREDIT + u + 1)
                if j == 0:
                    dve.wait_ge(rows_in[0], 8)
                elif j % FC == 0:
                    dve.wait_ge(rows_in[(j // 4) % 2], 16 * i + 16 * (j // 8 + 1))
                dve.wait_ge(hi_done, CREDIT + u - NB + 1)
                dve.tensor_tensor(hm[j % NB][:, :], ge[j % NB][:, :],
                                  half(gate_rows[(j // 4) % 2], (j // FC) % 2), ALU.mult)\
                    .then_inc(gated, 1)

            def low(u, j):
                dve.wait_ge(hi_done, CREDIT + u + 1)
                dve.wait_ge(y_done, CREDIT + u - NB + 1)
                dve.tensor_tensor(h_lo[j % NB][:, :], hm[j % NB][:, :], h_hi[j % NB][:, :].bitcast(f32),
                                  ALU.subtract).then_inc(lo_done, 1)

            def units(i, last):
                for j in range(8):
                    if not (last and j == 7):
                        gate_unit(i, j + 1)
                    low(8 * i + j, j)

            gate_unit(0, 0)
            dve.wait_ge(first_rows_mm, 2)
            dve.tensor_copy(half(gate_rows[0], 1), bank[3][:, :]).then_inc(rows_in[0], 8)
            with dve.Fori(0, EXPERTS // 2 - 1) as i:
                units(i, False)
            units(EXPERTS // 2 - 1, True)

            def add_experts(h):
                dve.wait_ge(yN_mm, h + 1)
                dve.scalar_tensor_tensor(out=tiles(x3, h).rearrange("p t d -> p (t d)"), in0=bank[4 + h][:, :],
                                         scalar=tg[:, G_FFN0:G_FFN0 + 1],
                                         in1=tiles(x2, h).rearrange("p t d -> p (t d)"),
                                         op0=ALU.mult, op1=ALU.add).then_inc(x3_ready, 1)
                dve.wait_ge(x3_ready, h + 1)

            wide = [128, TILES * HEADS, HD]

            def q_less_max(h):
                dve.wait_ge(q_mm, h + 1)
                link(dve.tensor_reduce(qmax[h][:, :], by_head(bank[h]), X, ALU.max))
                dve.tensor_tensor(by_head(qe[h]), by_head(bank[h]), qmax[h][:, :].unsqueeze(2).broadcast_to(wide),
                                  ALU.subtract).then_inc(q_sub, 1)

            def nd(h, k):
                return nd_bank(h, k)[:, 0:TPB * (NUM + DEN)].rearrange("p (t c) -> p t c", c=NUM + DEN)

            def sums_inverted(h):
                for k in range(BPH):
                    dve.wait_ge(nd_mm, h * BPH + k + 1)
                    dve.reciprocal(inv[h][:, k * TPB:(k + 1) * TPB, :, :].rearrange("p t k a -> p t (k a)"),
                                   nd(h, k)[:, :, NUM:]).then_inc(inv_ready, 1)

            def attention(h):
                for t in range(TILES):
                    k = t // TPB
                    dve.wait_ge(inv_ready, h * BPH + k + 1)
                    n = step(dve.tensor_tensor(by_head(ao[h])[:, t * HEADS:(t + 1) * HEADS, :],
                                               nd(h, k)[:, t % TPB, 0:NUM].rearrange("p (a c) -> p a c", c=HD),
                                               inv[h][:, t, 0, :].unsqueeze(2).broadcast_to([128, HEADS, HD]),
                                               ALU.mult))
                return n

            def add_q(h, n):
                dve.wait_ge(dve_step, n)
                dve.wait_ge(qn_ready, h + 1)
                dve.tensor_tensor(ao[h], ao[h], qn[h][:, :], ALU.add).then_inc(ao_ready, 1)

            def add_linear_attention(h):
                dve.wait_ge(proj_mm, h + 1)
                dve.scalar_tensor_tensor(out=tiles(x4, h).rearrange("p t d -> p (t d)"), in0=bank[2 + h][:, :],
                                         scalar=tg[:, G_XATTN1:G_XATTN1 + 1],
                                         in1=tiles(x3, h).rearrange("p t d -> p (t d)"),
                                         op0=ALU.mult, op1=ALU.add).then_inc(x4_ready, 1)
                dve.wait_ge(x4_ready, h + 1)

            add_experts(0)
            statistics(x3, 0)
            add_experts(1)
            normalise(x3, 5)
            statistics(x3, 1)
            normalise(x3, 6)
            for k in range(BPH):
                dve.wait_ge(kv_mm, k + 1)
                dve.tensor_copy(kv_raw[:, k, :, :].rearrange("p h d -> p (h d)"),
                                bank[2 + k][:, 0:HALVES * (D + 1)]).then_inc(kv_raw_ready, 1)
            for h in range(HALVES):
                q_less_max(h)
            sums_inverted(0)
            add_q(0, attention(0))
            sums_inverted(1)
            add_q(1, attention(1))
            add_linear_attention(0)
            statistics(x4, 0)
            add_linear_attention(1)
            normalise(x4, 7)

            def tokens_max(column, t):
                step(dve.tensor_reduce(amax["x"][:, column:column + 1], t.rearrange("p t d -> p (t d)"),
                                       X, ALU.max, apply_absolute_value=True))

            statistics(x4, 1)
            dve.wait_ge(xn_ready, 7)
            dve.wait_ge(xn_act, 7)
            tokens_max(0, tiles(xn, 0))
            normalise(x4, 8)
            dve.wait_ge(xn_ready, 8)
            tokens_max(1, tiles(xn, 1)[:, 0:TILES // 2, :])
            dve.wait_ge(xn_act, 8)
            tokens_max(2, tiles(xn, 1)[:, TILES // 2:, :])

            def max_over(k, n):
                dve.wait_ge(dve_step, steps[0])
                dve.tensor_reduce(amax1[k][:, :], amax[k][:, 0:n], X, ALU.max).then_inc(amax_ready[k], 1)

            def multiplier(k):
                dve.wait_ge(gmax_ready[k], 1)
                link(dve.tensor_scalar(step_raw[k][:, :], gmax[k][:, :], 1.0 / QMAX, floor[k][:, :],
                                       ALU.mult, ALU.max))
                dve.reciprocal(mul[k][:, :], step_raw[k][:, :]).then_inc(mul_ready[k], 1)

            def product_of(out, a, b, n, c=None):
                dve.wait_ge(dve_step, n)
                return step(dve.tensor_scalar(out[:, :], a[:, :], b[:, :], c, ALU.mult,
                                              *(() if c is None else (ALU.mult,))))

            def scaled(out, a, b, n):
                dve.wait_ge(dve_step, n)
                return step(dve.tensor_scalar(out[:, :], a[:, :], b, None, ALU.mult))

            def product_max(k, n):
                if k == "g":
                    dve.wait_ge(gu_ready, n + 1)
                    unit_ = half(gq[:, n // HALVES, :], n % HALVES)
                else:
                    dve.wait_ge(gu_mm, IC * HALVES + n + 1)
                    unit_ = bank[n][:, :]
                step(dve.tensor_reduce(amax[k][:, n:n + 1], unit_, X, ALU.max, apply_absolute_value=True))

            def chunk_max(k, t, c, n):
                dve.wait_ge(dve_step, n)
                step(dve.tensor_reduce(amax[k][:, c:c + 1], t[:, c, :], X, ALU.max, apply_absolute_value=True))

            max_over("x", 3)
            dve.wait_ge(gmax_ready["x"], 1)
            link(dve.tensor_scalar(scale["x"][:, :], gmax["x"][:, :], 1.0 / QMAX, QMIN_SCALE, ALU.mult, ALU.max))
            dve.reciprocal(mul["x"][:, :], scale["x"][:, :]).then_inc(mul_ready["x"], 1)
            dve.wait_ge(mul_ready["x"], 1)
            n = scaled(floor["g"], mul["x"], QMIN_SCALE, steps[0])
            for h in range(HALVES):
                dve.wait_ge(xq_ready, h + 1)
                dve.tensor_copy(half(xhi, h), half(nx, h)).then_inc(nx_high, 1)
                dve.wait_ge(nx_high, h + 1)
                dve.tensor_tensor(half(xlo, h), half(nx, h), half(xhi, h).bitcast(f32), ALU.subtract)\
                    .then_inc(nx_ready, 1)
            for n in range(IC * HALVES):
                product_max("g", n)
            max_over("g", IC * HALVES)
            multiplier("g")
            dve.tensor_tensor(scale["g"][:, :], step_raw["g"][:, :], unit["g"][:, :], ALU.mult).then_inc(scale_ready, 1)

            def sigmoid_steps(c):
                dve.wait_ge(sg_ready, c + 1)
                return step(dve.tensor_scalar(sq[:, c, :], sg[:, c, :], SIG_STEPS, None, ALU.mult))

            def gate_product(c, n):
                if n:
                    dve.wait_ge(dve_step, n)
                return step(dve.tensor_tensor(pg[:, c, :], ng[:, c, :], sq[:, c, :], ALU.mult))

            product_max("u", 0)
            dve.wait_ge(scale_ready, 1)
            dve.wait_ge(mul_ready["g"], 1)
            n = scaled(unit["p"], scale["g"], 1.0 / SIG_STEPS, steps[0])
            n = product_of(per_scale["g"], mul["g"], per_unit["g"], n - 1)
            product_max("u", 1)
            n = scaled(per_unit["p"], per_scale["g"], SIG_STEPS, n)
            product_max("u", 2)
            scaled(floor["p"], per_unit["p"], QMIN_SCALE, n)
            n = sigmoid_steps(0)
            product_max("u", 3)
            n = gate_product(0, n)
            product_max("u", 4)
            chunk_max("p", pg, 0, n)
            product_max("u", 5)
            dve.wait_ge(sq_ready, 1)
            m = gate_product(1, None)
            max_over("u", IC * HALVES)
            chunk_max("p", pg, 1, m)
            dve.wait_ge(sq_ready, 2)
            m = gate_product(2, None)
            multiplier("u")
            chunk_max("p", pg, 2, m)
            max_over("p", IC)
            n = product_of(scale["u"], step_raw["u"], unit["u"], m)
            dve.wait_ge(mul_ready["u"], 1)
            product_of(per_scale["u"], mul["u"], per_unit["u"], m)
            multiplier("p")
            dve.wait_ge(mul_ready["p"], 1)
            last = [step(dve.tensor_scalar(n3[:, 0, :], pg[:, 0, :], mul["p"][:, :], None, ALU.mult))]
            n = product_of(scale["p"], step_raw["p"], unit["p"], steps[0] - 1)
            m = product_of(per_scale["p"], mul["p"], per_unit["p"], steps[0] - 2)
            dve.wait_ge(nu_ready, HALVES)
            dve.wait_ge(dve_step, last[0])

            def gated_up(c):
                return step(dve.tensor_tensor(og[:, c, :], n3[:, c, :], nu[:, c, :], ALU.mult))

            last = [gated_up(0)]
            n = product_of(unit["o"], scale["p"], scale["u"], n)
            m = product_of(per_unit["o"], per_scale["p"], per_scale["u"], m)
            for c in range(1, IC):
                dve.wait_ge(n3_ready, c)
                dve.wait_ge(nu_ready, HALVES * (c + 1))
                last.append(gated_up(c))
                if c == 1:
                    scaled(floor["o"], per_unit["o"], QMIN_SCALE, m)
                chunk_max("o", og, c - 1, last[c - 1])
            chunk_max("o", og, IC - 1, last[IC - 1])
            max_over("o", IC)
            multiplier("o")
            dve.tensor_scalar(tscale[:, :], step_raw["o"][:, :], unit["o"][:, :], tg[:, G_FFN1:G_FFN1 + 1],
                              ALU.mult, ALU.mult)
            dve.wait_ge(mul_ready["o"], 1)
            for n in range(IC * HALVES):
                c, h = n // HALVES, n % HALVES
                whole, hi = half(n4[:, c, :], h), half(o_hi[:, c, :], h)
                if n == 0:
                    link(dve.tensor_scalar(whole, half(og[:, c, :], h), mul["o"][:, :], None, ALU.mult))
                else:
                    dve.wait_ge(n4_ready, n)
                if h == 0:
                    dve.tensor_copy(hi, whole).then_inc(ohi_dve, 1)
                    dve.wait_ge(ohi_dve, c + 1)
                else:
                    dve.wait_ge(ohi_ready, c + 1)
                dve.tensor_tensor(half(o_lo[:, c, :], h), whole, hi.bitcast(f32), ALU.subtract)\
                    .then_inc(olo_ready, 1)
            dve.wait_ge(x4T_ready, HALVES)
            for h in range(HALVES):
                dve.wait_ge(dn_mm, h + 1)
                dve.scalar_tensor_tensor(out=half(res, h), in0=bank[6 + h][:, :], scalar=tscale[:, :],
                                         in1=half(x4T, h), op0=ALU.mult, op1=ALU.add).then_inc(res_ready, 1)

        @block.tensor
        def _(pe):
            pe.sem_inc(z_ready, CREDIT)
            pe.sem_inc(y_done, CREDIT)
            mm = pe.matmul

            def keep_warm(b, n):
                for _ in range(n):
                    mm(bank[b][:, 0:256], zero16[:, 0:128], zero16[:, 0:256], start=True, stop=True)

            WARM_XN = {1: (4, 2), 2: (4, 0), 3: (0, 0), 4: (1, 25), 5: (7, 0), 6: (7, 0), 7: (1, 4), 8: (1, 20)}

            def transposes(dst, src, h, which=range(TILES)):
                for t in which:
                    last = pe.transpose(dst[:, t * 128:(t + 1) * 128], src[:, h * TILES + t, :], ident[:, :])
                return last

            def normalised(dst, n):
                keep_warm(*WARM_XN[n])
                h = (n - 1) % HALVES
                pe.wait_ge(xn_ready, n)
                transposes(dst, xn, h, range(TILES // 2))
                pe.wait_ge(xn_act, n)
                transposes(dst, xn, h, range(TILES // 2, TILES)).then_inc(xT_mm, 1)

            def three(dst, whi, wlo, xh, xl, start, stop, low_ready=None):
                mm(dst, whi, xh, start=start, stop=False)
                mm(dst, wlo, xh, start=False, stop=False)
                if low_ready:
                    pe.wait_ge(*low_ready)
                return mm(dst, whi, xl, start=False, stop=stop)

            def bias_rows(dst, k):
                for part in (row_hi, row_lo):
                    mm(dst[:, :], ones_r[:, :], part[:, k, :].unsqueeze(1).broadcast_to([1, TILES, D]),
                       start=(part is row_hi), stop=False)

            def context_rows(dst, w, bias):
                mm(dst, ones[0:1, 0:128], bias.unsqueeze(1).broadcast_to([1, HALVES, D]), start=True, stop=False)
                for h in range(HALVES):
                    last = mm(dst[:, h * D:(h + 1) * D], A("ctxT", 256)[:, h * 128:(h + 1) * 128], w,
                              start=False, stop=(h == HALVES - 1))
                return last

            def score_bias(h):
                b = slice(h * BPH * CTX, (h + 1) * BPH * CTX)
                mm(bank[h][:, 0:TILES * CTX], A("bq", 1).broadcast_to([128, 128]),
                   kT[:, b].unsqueeze(1).broadcast_to([128, TPB, BPH * CTX]), start=True, stop=False)

            def score_products(h):
                s = bank[h][:, 0:TILES * CTX]
                pe.wait_ge(xT_ready, h + 1)
                for t in range(TILES):
                    b = h * BPH + t // TPB
                    slot = (t % TPB) * BPH + t // TPB
                    last = mm(s[:, slot * CTX:(slot + 1) * CTX], half(xT, h)[:, t * D:(t + 1) * D],
                              wqk[:, b * CTX:(b + 1) * CTX], start=False, stop=(t == TILES - 1))
                last.then_inc(s_mm, 1)

            def attend(h):
                pe.wait_ge(pr_ready, h + 1)
                for k in range(TPB):
                    last = pe.transpose(bank[2 + h][:, k * D:(k + 1) * D],
                                        sc[:, h, k * BPH:(k + 1) * BPH, :].rearrange("p b c -> p (b c)"),
                                        ident[:, :])
                last.then_inc(prT_mm, 1)
                keep_warm(5 + 2 * h, 3)
                pe.wait_ge(prT_ready, h + 1)
                for k in range(TPB):
                    for b in range(BPH):
                        rows_ = slice(b * CTX, (b + 1) * CTX)
                        last = mm(bank[4 + 2 * h + b][:, k * D:(k + 1) * D], prT[rows_, h, k, :], v0[rows_, h, :],
                                  start=True, stop=True)
                last.then_inc(pv_mm, 1)

            pe.wait_ge(zero_ready, 1)
            keep_warm(7, 15)
            pe.wait_ge(const_ready, 1)
            pe.wait_ge(row_in, 16)
            mm(bank[2][:, 0:4], ones[0:1, 0:128], R("g", 4), start=True, stop=True).then_inc(g_mm, 1)
            pe.wait_ge(pa_in, 16)
            mm(bank[0][:, 0:256], A("wkT", D), A("ctxT", 256), start=True, stop=True).then_inc(kT_mm, 1)
            keep_warm(7, 2)
            pe.wait_ge(kT_ready, 1)
            mm(bank[5][:, 0:256], A("wq", D), kT[:, :], start=True, stop=True).then_inc(wqk_mm, 1)
            normalised(bank[6], 1)
            score_bias(0)
            keep_warm(4, 1)
            pe.wait_ge(wqk_ready, 1)
            score_products(0)
            normalised(bank[7], 2)
            score_bias(1)
            context_rows(bank[3][:, 0:256], A("wvT", D), R("bv0")).then_inc(v0_mm, 1)
            score_products(1)
            pe.wait_ge(tg_ready, 1)
            pe.wait_ge(v0_ready, 1)
            attend(0)
            attend(1)
            pe.wait_ge(pb_in, 16)
            context_rows(bank[2][:, 0:256], B("wkT"), R("bk1"))
            context_rows(bank[2][:, 256:512], B("wvT"), R("bv1")).then_inc(kv1_mm, 1)
            for h in range(HALVES):
                pe.wait_ge(s_sub, h + 1)
                if h == 0:
                    keep_warm(0, 20)
                normalised(bank[h], 3 + h)

            def logits(h):
                pe.wait_ge(xlo_ready, h + 1)
                for t in range(TILES):
                    k = slice(h * HT + t * D, h * HT + (t + 1) * D)
                    at = t * EXPERTS
                    last = three(bank[2 + h][:, at:at + EXPERTS], xhi[:, k], xlo[:, k], rw_hi[:, :], rw_lo[:, :],
                                 True, True)
                last.then_inc(lg_mm, 1)

            def z_unit(u, j, e):
                odd, h, c = (j // 4) % 2, (j // 2) % 2, j % 2
                if j % 4 == 0:
                    pe.wait_ge(w1_split, e + 1)
                pe.wait_ge(gelu_done, CREDIT + u - NB + 1)
                k = slice(c * D, (c + 1) * D)
                three(bank[4 + j % NB][:, :], w_hi[odd][:, k], w_lo[odd][:, k], half(xhi, h), half(xlo, h),
                      True, True).then_inc(z_ready, 1)

            def y_unit(u, j, e, last):
                odd, h, c = (j // 4) % 2, (j // 2) % 2, j % 2
                if j % 4 == 0:
                    pe.wait_ge(w2_split, e + 1)
                pe.wait_ge(hi_done, CREDIT + u + 1)
                k = slice(256 + c * D, 256 + (c + 1) * D)
                b = j % NB
                three(bank[h][:, :], w_hi[odd][:, k], w_lo[odd][:, k], h_hi[b][:, :], h_lo[b][:, :],
                      False, last and j // 4 == 1 and c == 1, (lo_done, CREDIT + u + 1)).then_inc(y_done, 1)

            def experts_to_tokens(h):
                pe.wait_ge(yT_ready, h + 1)
                for t in range(TILES):
                    last = pe.transpose(bank[4 + h][:, t * D:(t + 1) * D], half(yT, h)[:, t * D:(t + 1) * D],
                                        ident[:, :])
                last.then_inc(yN_mm, 1)

            def units(i, last):
                for j in range(8):
                    if last and j == 7:
                        experts_to_tokens(0)
                    if not (last and j >= 5):
                        z_unit(8 * i + j + 3, j + 3, 2 * i + (j + 3) // 4)
                    y_unit(8 * i + j, j, 2 * i + j // 4, last)

            def gate_columns(h):
                pe.wait_ge(lg_read, h + 1)
                pe.wait_ge(gate_ready, h + 1)
                for t in range(TILES):
                    last = pe.transpose(bank[2 + h][0:EXPERTS, t * D:(t + 1) * D], gate_[:, h * TILES + t, :],
                                        ident[:, :])
                last.then_inc(gateT_mm, 1)

            def first_rows(h):
                pe.wait_ge(gateT_ready[h], 1)
                mm(bank[2 + h][:, :], first_row[:, :], half(gateT, h), start=True, stop=True).then_inc(first_rows_mm, 1)

            pe.wait_ge(rw_ready, 1)
            pe.wait_ge(k1_ready, 1)
            logits(0)
            z_unit(0, 0, 0)
            logits(1)
            z_unit(1, 1, 0)
            for h in range(HALVES):
                mm(bank[h][:, :], zero16[:, 0:128], zero16[:, :], start=True, stop=False)

            gate_columns(0)
            z_unit(2, 2, 0)

            keep_warm(7, 2)
            gate_columns(1)
            first_rows(0)
            keep_warm(7, 8)
            first_rows(1)
            keep_warm(7, 2)
            with pe.Fori(0, EXPERTS // 2 - 1) as i:
                units(i, False)
            units(EXPERTS // 2 - 1, True)

            def key_products():
                pe.wait_ge(k1_soft, 3)
                for k in range(BPH):
                    rows_ = slice(k * CTX, (k + 1) * CTX)
                    for h in range(HALVES):
                        last = mm(bank[2 + k][:, h * (D + 1):(h + 1) * (D + 1)], k1[rows_, h, :], v1[rows_, h, :],
                                  start=True, stop=True)
                    last.then_inc(kv_mm, 1)

            pe.wait_ge(wb_ready, 1)
            for c in range(IC):
                if c == 2:
                    experts_to_tokens(1)
                if c >= 2:
                    keep_warm(6, 4)
                    pe.wait_ge(wT_ready, c - 1)
                for k in range(IC):
                    last = pe.transpose(bank[2 + c % 2][:, k * D:(k + 1) * D], wb_i[:, IC * c + k, :], ident[:, :])
                last.then_inc(wT_mm, 1)
            for h in range(HALVES):
                bias_rows(bank[h], 0)
            keep_warm(6, 7)
            for h in range(HALVES):
                normalised(bank[6 + h], 5 + h)
                if h == 0:
                    pe.wait_ge(wT_ready, IC)
                    key_products()
                pe.wait_ge(xT_ready, 3 + h)
                for t in range(TILES):
                    last = mm(bank[h][:, t * D:(t + 1) * D], half(xT, h)[:, t * D:(t + 1) * D], B("wqT"),
                              start=False, stop=(t == TILES - 1))
                last.then_inc(q_mm, 1)
            pe.wait_ge(x3_ready, HALVES)
            for h in range(HALVES):
                pe.wait_ge(qe_ready, h + 1)
                for t in range(TILES):
                    last = pe.transpose(bank[4 + h][:, t * D:(t + 1) * D], qe[h][:, t * D:(t + 1) * D], ident[:, :])
                last.then_inc(qeT_mm, 1)
                if h == 0:
                    keep_warm(7, 3)
                else:
                    pe.wait_ge(kv_raw_ready, BPH)
                    for k in range(HALVES):
                        bias_rows(bank[2 + k], 1)
                pe.wait_ge(kv_ready, 1)
                pe.wait_ge(qeT_ready, h + 1)
                for t in range(TILES):
                    at = (t % TPB) * (NUM + DEN)
                    last = mm(nd_bank(h, t // TPB)[:, at:at + NUM + DEN], qeT[h][:, t * D:(t + 1) * D],
                              kv[:, h * BPH + t // TPB, :], start=True, stop=True)
                    if t % TPB == TPB - 1:
                        last.then_inc(nd_mm, 1)
            for h in range(HALVES):
                keep_warm(5, 2 * h)
                pe.wait_ge(ao_ready, h + 1)
                for t in range(TILES):
                    last = pe.transpose(bank[4 + h][:, t * D:(t + 1) * D], ao[h][:, t * D:(t + 1) * D], ident[:, :])
                last.then_inc(aoT_mm, 1)
                keep_warm(5 - h, 3)
                pe.wait_ge(aoT_ready, h + 1)
                for t in range(TILES):
                    last = mm(bank[2 + h][:, t * D:(t + 1) * D], aoT[h][:, t * D:(t + 1) * D], B("wpT"),
                              start=False, stop=(t == TILES - 1))
                last.then_inc(proj_mm, 1)
            for h in range(HALVES):
                keep_warm(1, 3)
                pe.wait_ge(x4_ready, h + 1)
                transposes(bank[4 + h], x4, h).then_inc(x4T_mm, 1)
            for h in range(HALVES):
                normalised(bank[6 + h], 7 + h)

            keep_warm(1, 20)
            pe.wait_ge(wT_split, IC)
            pe.wait_ge(x4T_ready, HALVES)
            for n in range(2 * IC * HALVES):
                c, h = n // HALVES, n % HALVES
                w = c + IC if c < IC else c - IC
                if n < HALVES:
                    pe.wait_ge(nx_high, h + 1)
                if n >= IC * HALVES:
                    pe.wait_ge(gu_ready, n - IC * HALVES + 1)
                three(bank[n % (IC * HALVES)][:, :], wT_hi[:, w, :], wT_lo[:, w, :], half(xhi, h), half(xlo, h),
                      True, True, (nx_ready, h + 1)).then_inc(gu_mm, 1)
            pe.wait_ge(n3_ready, IC - 1)
            keep_warm(6, 24)
            pe.wait_ge(amax_ready["o"], 1)
            keep_warm(6, 20)
            for n in range(IC * HALVES):
                c, h = n // HALVES, n % HALVES
                pe.wait_ge((ohi_dve, ohi_ready)[h], c + 1)
                last = three(bank[6 + h][:, :], wT_hi[:, 2 * IC + c, :], wT_lo[:, 2 * IC + c, :],
                             half(o_hi[:, c, :], h), half(o_lo[:, c, :], h), c == 0, c == IC - 1,
                             (olo_ready, n + 1))
                if c == IC - 1:
                    last.then_inc(dn_mm, 1)


def kernel(**inputs):
    import concourse.bacc as _bacc
    from concourse import mybir as _mybir
    from concourse.bass_utils import run_bass_kernel_spmd as _run

    a = {k: np.asarray(v) for k, v in inputs.items()}

    def chunks(w):
        return w.reshape(-1, D, w.shape[1]).transpose(1, 0, 2)

    packa = np.concatenate([a["L0_xattn_Wq"], a["L0_xattn_Wk"].T, a["L0_xattn_Wv"].T,
                            a["ctx_1024"].reshape(BATCH * CTX, D).T, a["L0_ffn_router_w"].T,
                            a["L0_xattn_bq"][:, None], a["L0_xattn_bk"][:, None]], axis=1)
    packb = np.concatenate([a[f"L1_xattn_W{k}"].T for k in "qkvp"], axis=1)
    rows = np.concatenate([a["L0_xattn_bv"], a["L1_xattn_bq"], a["L1_xattn_bk"], a["L1_xattn_bv"],
                           a["L1_xattn_bp"], a["g_xattn"], a["g_ffn"]])[None]
    w1 = a["L0_ffn_w1"].transpose(2, 0, 1)
    w2 = a["L0_ffn_w2"].transpose(2, 0, 1).reshape(FC, D, EXPERTS, D).transpose(1, 2, 0, 3)
    experts = np.concatenate([w1, w2.reshape(D, EXPERTS, FC * D)], axis=2).reshape(D, -1)
    lpbq = np.concatenate([chunks(a["L1_ffn_w_up"]), chunks(a["L1_ffn_w_gate"]),
                           a["L1_ffn_w_down"].reshape(D, IC, D)], axis=1)
    arrays = {"in_x": a["x"], "in_packa": packa, "in_packb": packb, "in_rows": rows,
              "in_experts": experts, "in_lpbq": lpbq}
    arrays = {k: np.ascontiguousarray(v) for k, v in arrays.items()}
    nc = _bacc.Bacc("TRN2", target_bir_lowering=False, num_devices=1)
    args = [nc.dram_tensor(k, v.shape, _mybir.dt.from_np(v.dtype), kind="ExternalInput").ap()
            for k, v in arrays.items()]
    out = nc.dram_tensor("out", (D, TOKENS), _mybir.dt.float32, kind="ExternalOutput").ap()
    gates = nc.dram_tensor("gates", (EXPERTS, TOKENS), _mybir.dt.float32).ap()
    build(nc, *args, gates, out)
    r = _run(nc, [arrays], core_ids=[0])
    return np.ascontiguousarray(r.results[0]["out"].T).reshape(BATCH, SEQ, D)
```
